# Optimizing a Trainium2 kernel written in Bass

```python
import numpy as np
import jax
import jax.numpy as jnp

def _softmax(x, axis=-1):
    return jax.nn.softmax(x, axis=axis)

def _gelu(x):
    return jax.nn.gelu(x, approximate=True)

def _silu(x):
    return jax.nn.silu(x)

def _sigmoid(x):
    return jax.nn.sigmoid(x)

def _layernorm(x, axis=-1, eps=1e-05):
    m = jnp.mean(x, axis=axis, keepdims=True)
    v = jnp.var(x, axis=axis, keepdims=True)
    return (x - m) / jnp.sqrt(v + eps)

def _scatter_add(tgt, idx, src, axis=0):
    return tgt.at[idx].add(src)

def _segment_sum(src, seg, n):
    return jax.ops.segment_sum(src, seg, n)
kernel_name = 'mk_flamingo_gated_d1_seqx_r4_6496de'

def setup_inputs(seed: int=0):
    np.random.seed(seed)
    _w = jnp.asarray

    def _rec_inputs():
        import jax
        import jax.numpy as jnp
        _rk = jax.random.key(seed)
        x = 7.22e-05 + 1 * jax.random.normal(jax.random.fold_in(_rk, 1), (4, 512, 256), jnp.float32)
        _lenS = 512 - jax.random.randint(jax.random.fold_in(_rk, 7), (4,), 0, max(1, 512 // 4) + 1, jnp.int32)
        _lenS2 = 1601 - jax.random.randint(jax.random.fold_in(_rk, 8), (4,), 0, max(1, 1601 // 4) + 1, jnp.int32)
        _ctx_1024P = jax.random.normal(jax.random.fold_in(_rk, 11), (4, 16, 256), jnp.float32)
        _ctx_1024c = jax.random.dirichlet(jax.random.fold_in(_rk, 511), 0.3 * jnp.ones((16,), jnp.float32), (4, 1601))
        _ctx_1024t = jnp.einsum('bsk,bkd->bsd', _ctx_1024c, _ctx_1024P)
        _ctx_1024t = _ctx_1024t * jax.lax.rsqrt(jnp.mean(jnp.square(_ctx_1024t)) + 1e-12) * 0.953939
        ctx_1024 = 4.13588e-05 + 0.999923 * (_ctx_1024t + 0.3 * jax.random.normal(jax.random.fold_in(_rk, 611), (4, 1601, 256), jnp.float32))
        _validS = jnp.arange(512)[None, :] < _lenS[:, None]
        _validS2 = jnp.arange(1601)[None, :] < _lenS2[:, None]
        _causal = jnp.tril(jnp.ones((512, 512), dtype=bool))
        mask_BxSxS2_ik1 = jnp.where(jnp.broadcast_to(_validS2[:, None, :], (4, 512, 1601)), 1, 0).astype(jnp.int32)
        _g = jax.random.normal(jax.random.fold_in(_rk, 9001), (2, 1), jnp.float32)
        _g = jnp.sign(_g) * jnp.maximum(jnp.abs(_g), 1.0) + (_g == 0) * 1.0
        g_xattn = _g[0]
        g_ffn = _g[1]
        return (x, ctx_1024, mask_BxSxS2_ik1, g_xattn, g_ffn)
    x, ctx_1024, mask_BxSxS2_ik1, g_xattn, g_ffn = _rec_inputs()

    def _L0_xattn_setup():
        import jax, jax.numpy as jnp
        import numpy as np
        HID = 256
        HEADS = 16
        HEAD_DIM = HID // HEADS

        def _split_heads(x, W, b):
            B, S, _ = x.shape
            y = x @ W + b
            return y.reshape(B, S, HEADS, HEAD_DIM).transpose(0, 2, 1, 3)
        key = jax.random.key(seed)
        ks = jax.random.split(key, 12)
        B, S = (4, 512)
        inp = {'query': jax.random.normal(ks[0], (B, S, HID), dtype=jnp.float32), 'key': jax.random.normal(ks[1], (B, S, HID), dtype=jnp.float32), 'value': jax.random.normal(ks[2], (B, S, HID), dtype=jnp.float32), 'mask': jax.random.randint(ks[3], (B, S, S), 0, 2, dtype=jnp.int32), 'Wq': jax.random.normal(ks[4], (HID, HID), dtype=jnp.float32) * (1.0 / np.sqrt(HID)), 'bq': jnp.zeros((HID,), dtype=jnp.float32), 'Wk': jax.random.normal(ks[5], (HID, HID), dtype=jnp.float32) * (1.0 / np.sqrt(HID)), 'bk': jnp.zeros((HID,), dtype=jnp.float32), 'Wv': jax.random.normal(ks[6], (HID, HID), dtype=jnp.float32) * (1.0 / np.sqrt(HID)), 'bv': jnp.zeros((HID,), dtype=jnp.float32), 'Wo': jax.random.normal(ks[7], (HID, HID), dtype=jnp.float32) * (1.0 / np.sqrt(HID)), 'bo': jnp.zeros((HID,), dtype=jnp.float32)}
        return inp
    _L0_xattn_all = _L0_xattn_setup()
    _L0_xattn_in = {k: v for k, v in _L0_xattn_all.items() if k in ('Wq', 'bq', 'Wk', 'bk', 'Wv', 'bv', 'Wo', 'bo')}
    del _L0_xattn_all

    def _L0_ffn_setup():
        import jax, jax.numpy as jnp
        import numpy as np

        def _binarize(w):
            alpha = jax.lax.stop_gradient(jnp.mean(jnp.abs(w), axis=1, keepdims=True))
            bw = alpha * jnp.sign(w)
            return w + jax.lax.stop_gradient(bw - w)
        key = jax.random.key(seed)
        k1, k2, k3, k4, k5 = jax.random.split(key, 5)
        D, H = (256, 1024)
        x = jax.random.normal(k1, (64, 196, D), dtype=jnp.float32)
        w1 = jax.random.normal(k2, (H, D), dtype=jnp.float32) * 0.02
        b1 = jax.random.normal(k3, (H,), dtype=jnp.float32) * 0.02
        w2 = jax.random.normal(k4, (D, H), dtype=jnp.float32) * 0.02
        b2 = jax.random.normal(k5, (D,), dtype=jnp.float32) * 0.02
        return {'x': x, 'w1': w1, 'b1': b1, 'w2': w2, 'b2': b2}
    _L0_ffn_all = _L0_ffn_setup()
    _L0_ffn_in = {k: v for k, v in _L0_ffn_all.items() if k in ('w1', 'b1', 'w2', 'b2')}
    del _L0_ffn_all
    return {'x': x, 'ctx_1024': ctx_1024, 'mask_BxSxS2_ik1': mask_BxSxS2_ik1, 'g_xattn': g_xattn, 'g_ffn': g_ffn, 'L0_xattn_Wq': _L0_xattn_in['Wq'], 'L0_xattn_bq': _L0_xattn_in['bq'], 'L0_xattn_Wk': _L0_xattn_in['Wk'], 'L0_xattn_bk': _L0_xattn_in['bk'], 'L0_xattn_Wv': _L0_xattn_in['Wv'], 'L0_xattn_bv': _L0_xattn_in['bv'], 'L0_xattn_Wo': _L0_xattn_in['Wo'], 'L0_xattn_bo': _L0_xattn_in['bo'], 'L0_ffn_w1': _L0_ffn_in['w1'], 'L0_ffn_b1': _L0_ffn_in['b1'], 'L0_ffn_w2': _L0_ffn_in['w2'], 'L0_ffn_b2': _L0_ffn_in['b2']}

def reference(x, ctx_1024, mask_BxSxS2_ik1, g_xattn, g_ffn, L0_xattn_Wq, L0_xattn_bq, L0_xattn_Wk, L0_xattn_bk, L0_xattn_Wv, L0_xattn_bv, L0_xattn_Wo, L0_xattn_bo, L0_ffn_w1, L0_ffn_b1, L0_ffn_w2, L0_ffn_b2):
    import jax
    import jax.numpy as jnp

    def _L0_xattn_ref(query, key, value, mask, Wq, bq, Wk, bk, Wv, bv, Wo, bo):
        import jax, jax.numpy as jnp
        import numpy as np
        HID = 256
        HEADS = 16
        HEAD_DIM = HID // HEADS

        def _split_heads(x, W, b):
            B, S, _ = x.shape
            y = x @ W + b
            return y.reshape(B, S, HEADS, HEAD_DIM).transpose(0, 2, 1, 3)
        B, S, _ = query.shape
        Q = _split_heads(query, Wq, bq)
        K = _split_heads(key, Wk, bk)
        V = _split_heads(value, Wv, bv)
        scale = 1.0 / jnp.sqrt(jnp.asarray(HEAD_DIM, dtype=Q.dtype))
        energy = jnp.einsum('bhqd,bhkd->bhqk', Q, K) * scale
        m = mask[:, None, :, :]
        energy = jnp.where(m == 0, jnp.asarray(-1000000000.0, dtype=energy.dtype), energy)
        attn = jax.nn.softmax(energy, axis=-1)
        out = jnp.einsum('bhqk,bhkd->bhqd', attn, V)
        out = out.transpose(0, 2, 1, 3).reshape(B, S, HID)
        return out @ Wo + bo

    def _L0_ffn_ref(x, w1, b1, w2, b2):
        import jax, jax.numpy as jnp
        import numpy as np

        def _binarize(w):
            alpha = jax.lax.stop_gradient(jnp.mean(jnp.abs(w), axis=1, keepdims=True))
            bw = alpha * jnp.sign(w)
            return w + jax.lax.stop_gradient(bw - w)
        bw1 = _binarize(w1)
        h = jnp.einsum('bsd,hd->bsh', x, bw1) + b1
        h = jax.nn.gelu(h, approximate=False)
        bw2 = _binarize(w2)
        out = jnp.einsum('bsh,dh->bsd', h, bw2) + b2
        return out
    x = x + jnp.tanh(g_xattn[0]) * _L0_xattn_ref(_layernorm(x, axis=-1), ctx_1024, ctx_1024, mask_BxSxS2_ik1, L0_xattn_Wq, L0_xattn_bq, L0_xattn_Wk, L0_xattn_bk, L0_xattn_Wv, L0_xattn_bv, L0_xattn_Wo, L0_xattn_bo)
    x = x + jnp.tanh(g_ffn[0]) * _L0_ffn_ref(_layernorm(x, axis=-1), L0_ffn_w1, L0_ffn_b1, L0_ffn_w2, L0_ffn_b2)
    return x

_drawn_inputs = setup_inputs


def setup_inputs(seed=0):
    import zlib

    import numpy as np

    out = dict(_drawn_inputs(seed))
    spreads = {'L0_xattn_bq': (0.0, 0.48),
     'L0_xattn_bk': (0.0, 0.8),
     'L0_xattn_bv': (0.0, 0.1),
     'L0_xattn_bo': (0.0, 0.1)}
    factors = {'L0_ffn_b1': 8.0, 'L0_ffn_b2': 3.345}
    for name, (base, spread) in spreads.items():
        noise = np.random.default_rng([zlib.crc32(name.encode()), seed]).standard_normal(out[name].shape)
        drawn = base * np.exp(spread * noise) if base else spread * noise
        out[name] = jnp.asarray(drawn.astype(out[name].dtype))
    for name, factor in factors.items():
        out[name] = (out[name] * factor).astype(out[name].dtype)
    return out
```

```python
from contextlib import ExitStack

import concourse.bass as bass
from concourse import mybir

ALU = mybir.AluOpType
ACT = mybir.ActivationFunctionType
AX_X = mybir.AxisListType.X
F32 = mybir.dt.float32
BF16 = mybir.dt.bfloat16
I32 = mybir.dt.int32

P = 128
B, S, D = 4, 512, 256
SK = 1601
H, DH = 16, 16
F = 1024
DC = D // P
QT = S // P
FC = F // P
KT = -(-SK // P)
KLAST = SK - (KT - 1) * P
HG = 4
NG = H // HG
GR = HG * DH
PARTS = 3
SCALE = float(DH) ** -0.5
MASKED = -(2.0 ** 100)
LOWEST = -3.0e38
LN_EPS = 1e-5

STACK = [(0, 0, 0), (32, 0, 1), (48, 0, 2), (64, 1, 0), (80, 1, 1), (96, 2, 0)]
MAX_ROW = 112

KEY_BLOCKS = [(k, min(512, SK - k)) for k in range(0, SK, 512)]
NCH = 4
CW = -(-SK // NCH)
CHUNKS = [(c * CW, min(CW, SK - c * CW)) for c in range(NCH)]


def keys_in(kt):
    return KLAST if kt == KT - 1 else P


def layernorm_scales(nc, v, mean_var, rstd, var_ready, std_ready, step, base, index):
    nc.vector.tensor_scalar(rstd[:, :, 0], mean_var[:, :, 1], LN_EPS, None, ALU.add).then_inc(var_ready, 1)
    v.wait_ge(std_ready, index + 1)
    nc.vector.reciprocal(rstd[:, :, 1], rstd[:, :, 0]).then_inc(step, 1)
    v.wait_ge(step, base)


def prepare(nc, w, x, ctx_in, mask, wq, bq, wk, bk, wv, bv, w1, w2, kparts_d, qparts_d, values_d, bias_d, biasT_d):
    with ExitStack() as es:
        def sb(name, shape, dt=F32):
            return es.enter_context(nc.sbuf_tensor(name, shape, dt))

        def sem(name):
            return es.enter_context(nc.semaphore(name))

        wq_s, wk_s, wv_s = sb("wq_s", [P, DC, D]), sb("wk_s", [P, DC, D]), sb("wv_s", [P, DC, D])
        bq_s, bk_s, bv_s = sb("bq_s", [P, DC]), sb("bk_s", [P, DC]), sb("bv_s", [P, D])
        x_s, xn, xT = sb("x_s", [P, QT, D]), sb("xn", [P, QT, D]), sb("xT", [P, DC, S])
        stats, mean_var, rstd = sb("stats", [P, QT, 6]), sb("mean_var", [P, QT, 2]), sb("rstd", [P, QT, 2])
        c_s, cT = sb("c_s", [P, KT, D]), sb("cT", [P, DC, SK])
        kp, krest = sb("kp", [P, PARTS, DC, SK], BF16), sb("krest", [P, DC, SK])
        qp, qrest = sb("qp", [P, PARTS, DC, S], BF16), sb("qrest", [P, DC, S])
        vals = sb("vals", [P, KT, H, 2 * DH])
        m_s, bias, biasT = sb("m_s", [P, 2, SK], I32), sb("bias", [P, QT, SK], BF16), sb("biasT", [P, KT, S], BF16)
        w1_s = cT[:, :, :].rearrange("p a b -> p (a b)")[:, 0:FC * D].rearrange("p (c d) -> p c d", c=FC)
        w2_s = krest[:, :, :].rearrange("p a b -> p (a b)")[:, 0:DC * F].rearrange("p (c d) -> p c d", c=DC)
        a1, a2 = sb("a1", [P, FC]), sb("a2", [P, DC])
        ps = es.enter_context(nc.psum_tensor("ps1", [P, 8, 512], F32))
        psb = ps[:, :, :].bitcast(BF16)

        weights_in, ffn_in = sem("weights_in"), sem("ffn_in")
        ident_step, consts_ready = sem("ident_step"), sem("consts_ready")
        alpha_sum, alpha_ready, sign_ready = sem("alpha_sum"), sem("alpha_ready"), sem("sign_ready")
        ffn_scaled, ffn_tr, ffn_kept = sem("ffn_scaled"), sem("ffn_tr"), sem("ffn_kept")
        x_in, c_in, m_in = sem("x_in"), sem("c_in"), [sem("m_in0"), sem("m_in1")]
        ln_step, var_ready, std_ready, xn_ready = sem("ln_step"), sem("var_ready"), sem("std_ready"), sem("xn_ready")
        filled, act_freed, dve_freed = sem("filled"), sem("act_freed"), sem("dve_freed")
        hi_ready, rest_ready, mid_ready, lo_ready = sem("hi_ready"), sem("rest_ready"), sem("mid_ready"), sem("lo_ready")
        bias_ready, wait_carrier = sem("bias_ready"), sem("wait_carrier1")
        qk_out, v_out, bias_out, biasT_out = sem("qk_out"), sem("v_out"), sem("bias_out"), sem("biasT_out")

        jobs = [("cT", c, kb) for kb in range(len(KEY_BLOCKS)) for c in range(DC)]
        jobs += [("xT", c, 0) for c in range(DC)]
        jobs += [("q", m, 0) for m in range(DC)]
        jobs += [("k", m, kb) for m in range(DC) for kb in range(len(KEY_BLOCKS))]
        pairs = list(range(0, KT, 2))
        for kt in pairs:
            jobs += [("v", kt, 0), ("m", kt, 0)]
        jobs_act = [j for j in jobs if j[0] in ("cT", "xT", "m")]
        jobs_dve = [j for j in jobs if j[0] in ("q", "k", "v")]
        splits = [j for j in jobs if j[0] in ("q", "k")]
        NJ, NA, NV, NS = len(jobs), len(jobs_act), len(jobs_dve), len(splits)

        def operand(kind, m, kb):
            if kind == "q":
                return qp, qrest, bq_s, m, 0, S
            return kp, krest, bk_s, m, KEY_BLOCKS[kb][0], KEY_BLOCKS[kb][1]

        with nc.Block() as block:
            @block.sync
            def _(sp):
                sp.dma_start(w1_s, w1.rearrange("(c p) d -> p c d", p=P)).then_inc(ffn_in, 16)
                sp.dma_start(w2_s, w2.rearrange("(c p) d -> p c d", p=P)).then_inc(ffn_in, 16)
                for dst, src in ((wq_s, wq), (wk_s, wk), (wv_s, wv)):
                    sp.dma_start(dst[:, :, :], src.rearrange("(c p) d -> p c d", p=P)).then_inc(weights_in, 16)
                for dst, src in ((bq_s, bq), (bk_s, bk)):
                    sp.dma_start(dst[:, :], src.rearrange("(c p) -> p c", p=P), allow_slow_non_contiguous=True).then_inc(weights_in, 16)
                sp.dma_start(bv_s[:, :], bv.rearrange("(a d) -> a d", a=1).to_broadcast([P, D])).then_inc(weights_in, 16)
                def batch(b):
                    sp.wait_ge(xn_ready, b * QT)
                    sp.dma_start(x_s[:, :, :], x[b, :, :].rearrange("(t p) d -> p t d", p=P)).then_inc(x_in, 16)
                    sp.wait_ge(filled, b * NJ)
                    sp.dma_start(c_s[:, 0:KT - 1, :], ctx_in[b, 0:(KT - 1) * P, :].rearrange("(t p) d -> p t d", p=P)).then_inc(c_in, 16)
                    sp.dma_start(c_s[0:KLAST, KT - 1, :], ctx_in[b, (KT - 1) * P:SK, :]).then_inc(c_in, 16)
                    for qt in range(QT):
                        if qt >= 2:
                            sp.wait_ge(bias_ready, b * QT + qt - 1)
                        else:
                            sp.wait_ge(bias_ready, b * QT)
                        sp.dma_start(m_s[:, qt % 2, :], mask[b, qt * P:(qt + 1) * P, :]).then_inc(m_in[qt % 2], 16)

                batch(0)
                with nc.sync.Fori(1, B) as b:
                    batch(b)

            @block.gpsimd
            def _(pool):
                nc.gpsimd.memset(w["ident"][:, :], 0.0).then_inc(ident_step, 1)
                nc.gpsimd.memset(w["ident16"][:, :], 0.0).then_inc(ident_step, 1)
                nc.gpsimd.memset(vals[:, :, :, :], 1.0).then_inc(consts_ready, 1)
                nc.gpsimd.memset(biasT[:, KT - 1, :], 0.0).then_inc(consts_ready, 1)
                pool.wait_ge(ident_step, 2)
                for m in (w["ident"], w["ident16"]):
                    nc.gpsimd.affine_select(out=m[:, :], in_=m[:, :], compare_op=ALU.not_equal, fill=1.0, base=0,
                                            pattern=[[-1, P]], channel_multiplier=1).then_inc(consts_ready, 1)
                def batch(b):
                    for n, (kind, m, kb) in enumerate(splits):
                        parts, rest, _, m, c0, cn = operand(kind, m, kb)
                        pool.wait_ge(mid_ready, b * NS + n + 1)
                        nc.gpsimd.tensor_tensor(parts[:, 2, m, c0:c0 + cn], rest[:, m, c0:c0 + cn],
                                                parts[:, 1, m, c0:c0 + cn], ALU.subtract).then_inc(lo_ready, 1)
                    pool.wait_ge(lo_ready, b * NS + NS)
                    for g in range(NG):
                        rows = slice(GR * (g % 2), GR * (g % 2) + GR)
                        for part in range(PARTS):
                            pool.dma_start(kparts_d[b * NG + g, part, :, :, :].rearrange("d h c -> h d c"),
                                           kp[rows, part, g // 2, :]).then_inc(qk_out, 16)
                            pool.dma_start(qparts_d[b * NG + g, part, :, :, :].rearrange("d h c -> h d c"),
                                           qp[rows, part, g // 2, :]).then_inc(qk_out, 16)
                    pool.wait_ge(dve_freed, b * NV + NV)
                    for g in range(NG):
                        pool.dma_start(values_d[b * NG + g, :, :, :].rearrange("p t c -> p t c"),
                                       vals[:, :, HG * g:HG * (g + 1), :].rearrange("p t h c -> p t (h c)")).then_inc(v_out, 16)
                    pool.wait_ge(bias_ready, b * QT + QT)
                    pool.dma_start(bias_d[b, :, :, :], bias[:, :, :]).then_inc(bias_out, 16)
                    pool.wait_ge(act_freed, b * NA + NA)
                    pool.dma_start(biasT_d[b, :, :, :], biasT[:, :, :]).then_inc(biasT_out, 16)

                batch(0)
                with nc.gpsimd.Fori(1, B) as b:
                    batch(b)
                pool.wait_ge(qk_out, B * NG * PARTS * 2 * 16)
                pool.wait_ge(v_out, B * NG * 16)
                pool.wait_ge(bias_out, B * 16)
                pool.wait_ge(biasT_out, B * 16)

            @block.scalar
            def _(act):
                act.wait_ge(ffn_in, 32)
                act.wait_ge(alpha_sum, 2)
                nc.scalar.activation(w1_s, w1_s, ACT.Sign).then_inc(sign_ready, 1)
                nc.scalar.activation(w2_s, w2_s, ACT.Sign).then_inc(sign_ready, 1)
                for n in range(2 * DC * 2):
                    act.wait_ge(ffn_tr, n + 1)
                    if n < 2 * DC:
                        dst = w["w1T"][:, n // 2, (n % 2) * 512:(n % 2 + 1) * 512]
                        src = ps[:, n, :]
                    else:
                        k = n - 2 * DC
                        dst, src = w["w2T"][:, 2 * k:2 * k + 2, :], ps[:, n, :].rearrange("p (a d) -> p a d", a=2)
                    nc.scalar.activation(dst, src, ACT.Copy).then_inc(ffn_kept, 1)
                def batch(b):
                    act.wait_ge(var_ready, b + 1)
                    nc.scalar.activation(rstd[:, :, 0], rstd[:, :, 0], ACT.Sqrt).then_inc(std_ready, 1)
                    n_split = 0

                    def round_mid(n):
                        kind, m, kb = splits[n]
                        parts, rest, _, m, c0, cn = operand(kind, m, kb)
                        act.wait_ge(rest_ready, b * NS + n + 1)
                        nc.scalar.activation(parts[:, 1, m, c0:c0 + cn], rest[:, m, c0:c0 + cn], ACT.Copy).then_inc(mid_ready, 1)

                    for n, (kind, i, kb) in enumerate(jobs):
                        bank = n % 8
                        if kind == "v":
                            continue
                        act.wait_ge(filled, b * NJ + n + 1)
                        if kind == "cT":
                            k0, kn = KEY_BLOCKS[kb]
                            nc.scalar.activation(cT[:, i, k0:k0 + kn], ps[:, bank, 0:kn], ACT.Copy).then_inc(act_freed, 1)
                        elif kind == "xT":
                            nc.scalar.activation(xT[:, i, :], ps[:, bank, :], ACT.Copy).then_inc(act_freed, 1)
                        elif kind == "m":
                            act.wait_ge(biasT_out, b * 16)
                            if i == 0:
                                act.wait_ge(consts_ready, 4)
                            if i == KT - 1:
                                nc.scalar.activation(biasT[0:KLAST, i, :], psb[0:KLAST, bank, 0:S], ACT.Copy).then_inc(act_freed, 1)
                            else:
                                nc.scalar.activation(biasT[:, i:i + 2, :], psb[:, bank, :].rearrange("p (a s) -> p a s", a=2),
                                                     ACT.Copy).then_inc(act_freed, 1)
                        else:
                            parts, rest, bias_s, m, c0, cn = operand(kind, i, kb)
                            if n_split == 0:
                                act.wait_ge(qk_out, b * NG * PARTS * 2 * 16)
                                act.wait_ge(weights_in, 6 * 16)
                            nc.scalar.activation(parts[:, 0, m, c0:c0 + cn], ps[:, bank, 0:cn], ACT.Identity,
                                                 bias=bias_s[:, m:m + 1]).then_inc(hi_ready, 1)
                            if n_split >= 1:
                                round_mid(n_split - 1)
                            n_split += 1
                            if n_split == NS:
                                round_mid(NS - 1)

                batch(0)
                with nc.scalar.Fori(1, B) as b:
                    batch(b)

            @block.vector
            def _(v):
                v.wait_ge(ffn_in, 32)
                nc.vector.tensor_reduce(a1[:, :], w1_s, AX_X, ALU.add, apply_absolute_value=True).then_inc(alpha_sum, 1)
                nc.vector.tensor_reduce(a2[:, :], w2_s, AX_X, ALU.add, apply_absolute_value=True).then_inc(alpha_sum, 1)
                v.wait_ge(alpha_sum, 2)
                nc.vector.tensor_scalar(a1[:, :], a1[:, :], 1.0 / D, None, ALU.mult).then_inc(alpha_ready, 1)
                nc.vector.tensor_scalar(a2[:, :], a2[:, :], 1.0 / F, None, ALU.mult).then_inc(alpha_ready, 1)
                v.wait_ge(alpha_ready, 2)
                v.wait_ge(sign_ready, 2)
                for c in range(FC):
                    nc.vector.tensor_scalar(w1_s[:, c, :], w1_s[:, c, :], a1[:, c:c + 1], None, ALU.mult).then_inc(ffn_scaled, 1)
                for c in range(DC):
                    nc.vector.tensor_scalar(w2_s[:, c, :], w2_s[:, c, :], a2[:, c:c + 1], None, ALU.mult).then_inc(ffn_scaled, 1)
                v.wait_ge(weights_in, 6 * 16)
                v.wait_ge(consts_ready, 4)
                def batch(b):
                    v.wait_ge(x_in, 16 * b + 16)
                    for t in range(QT):
                        nc.vector.bn_stats(stats[:, t, :], x_s[:, t, :]).then_inc(ln_step, 1)
                    v.wait_ge(ln_step, b * (2 * QT + 1) + QT)
                    v.sem_inc(wait_carrier, 1)
                    for t in range(QT):
                        nc.vector.bn_aggr(mean_var[:, t, :], stats[:, t, :]).then_inc(ln_step, 1)
                    v.wait_ge(ln_step, b * (2 * QT + 1) + 2 * QT)
                    layernorm_scales(nc, v, mean_var, rstd, var_ready, std_ready, ln_step, b * (2 * QT + 1) + 2 * QT + 1, b)
                    v.wait_ge(filled, b * NJ)
                    for t in range(QT):
                        nc.vector.tensor_scalar(xn[:, t, :], x_s[:, t, :], mean_var[:, t, 0:1], rstd[:, t, 1:2],
                                                ALU.subtract, ALU.mult).then_inc(xn_ready, 1)
                    v.wait_ge(bias_out, 16 * b)
                    converted = 0
                    n_split = 0
                    for n, (kind, i, kb) in enumerate(jobs):
                        bank = n % 8
                        if kind in ("q", "k"):
                            parts, rest, bias_s, m, c0, cn = operand(kind, i, kb)
                            v.wait_ge(hi_ready, b * NS + n_split + 1)
                            nc.vector.scalar_tensor_tensor(rest[:, m, c0:c0 + cn], ps[:, bank, 0:cn], bias_s[:, m:m + 1],
                                                           parts[:, 0, m, c0:c0 + cn], ALU.add, ALU.subtract).then_inc(rest_ready, 1)
                            v.wait_ge(rest_ready, b * NS + n_split + 1)
                            v.sem_inc(dve_freed, 1)
                            n_split += 1
                            if n_split % 2 == 0 and converted < QT:
                                v.wait_ge(m_in[converted % 2], (b * (QT // 2) + converted // 2 + 1) * 16)
                                nc.vector.tensor_scalar(bias[:, converted, :], m_s[:, converted % 2, :], 0, MASKED,
                                                        ALU.is_equal, ALU.mult).then_inc(bias_ready, 1)
                                converted += 1
                        elif kind == "v":
                            v.wait_ge(filled, b * NJ + n + 1)
                            v.wait_ge(v_out, b * NG * 16)
                            tiles = 2 if i < KT - 1 else 1
                            r = P if i < KT - 1 else KLAST
                            for t in range(tiles):
                                last = nc.vector.tensor_tensor(
                                    vals[0:r, i + t, :, 0:DH],
                                    ps[0:r, bank, t * D:(t + 1) * D].rearrange("p (h c) -> p h c", h=H),
                                    bv_s[0:r, :].rearrange("p (h c) -> p h c", h=H), ALU.add)
                                if t == tiles - 1:
                                    last.then_inc(dve_freed, 1)

                batch(0)
                with nc.vector.Fori(1, B) as b:
                    batch(b)

            @block.tensor
            def _(pe):
                pe.wait_ge(consts_ready, 4)
                pe.wait_ge(ffn_scaled, FC + DC)
                for n in range(2 * DC):
                    for q in range(4):
                        c = (n % 2) * 4 + q
                        last = nc.tensor.transpose(ps[:, n, q * P:(q + 1) * P], w1_s[:, c, (n // 2) * P:(n // 2 + 1) * P], w["ident"][:, :])
                    last.then_inc(ffn_tr, 1)
                for n in range(2 * DC):
                    for q in range(4):
                        f, c = 2 * n + q // 2, q % 2
                        last = nc.tensor.transpose(ps[:, 2 * DC + n, q * P:(q + 1) * P], w2_s[:, c, f * P:(f + 1) * P], w["ident"][:, :])
                    last.then_inc(ffn_tr, 1)
                pe.wait_ge(ffn_kept, 4 * DC)
                pe.wait_ge(weights_in, 6 * 16)
                def batch(b):
                    pe.wait_ge(act_freed, b * NA)
                    pe.wait_ge(dve_freed, b * NV)
                    for n, (kind, i, kb) in enumerate(jobs):
                        bank = n % 8
                        if n >= 8:
                            before = jobs[n - 8]
                            if before in jobs_act:
                                pe.wait_ge(act_freed, b * NA + jobs_act.index(before) + 1)
                            else:
                                pe.wait_ge(dve_freed, b * NV + jobs_dve.index(before) + 1)
                        if kind == "cT":
                            if n == 0:
                                pe.wait_ge(c_in, 32 * b + 32)
                            k0, kn = KEY_BLOCKS[kb]
                            for q in range(0, kn, P):
                                r = min(P, kn - q)
                                last = nc.tensor.transpose(ps[:, bank, q:q + r], c_s[0:r, (k0 + q) // P, i * P:(i + 1) * P],
                                                           w["ident"][0:r, 0:r])
                        elif kind == "xT":
                            pe.wait_ge(xn_ready, b * QT + QT)
                            for q in range(QT):
                                last = nc.tensor.transpose(ps[:, bank, q * P:(q + 1) * P], xn[:, q, i * P:(i + 1) * P], w["ident"][:, :])
                        elif kind == "q":
                            pe.wait_ge(act_freed, b * NA + jobs_act.index(("xT", DC - 1, 0)) + 1)
                            for c in range(DC):
                                last = nc.tensor.matmul(ps[:, bank, :], wq_s[:, c, i * P:(i + 1) * P], xT[:, c, :],
                                                        start=c == 0, stop=c == DC - 1)
                        elif kind == "k":
                            k0, kn = KEY_BLOCKS[kb]
                            for c in range(DC):
                                last = nc.tensor.matmul(ps[:, bank, 0:kn], wk_s[:, c, i * P:(i + 1) * P], cT[:, c, k0:k0 + kn],
                                                        start=c == 0, stop=c == DC - 1)
                        elif kind == "v":
                            for t in range(2 if i < KT - 1 else 1):
                                r = keys_in(i + t)
                                for c in range(DC):
                                    last = nc.tensor.matmul(ps[0:r, bank, t * D:(t + 1) * D], cT[:, c, (i + t) * P:(i + t) * P + r],
                                                            wv_s[:, c, :], start=c == 0, stop=c == DC - 1)
                        else:
                            pe.wait_ge(bias_ready, b * QT + QT)
                            for t in range(2 if i < KT - 1 else 1):
                                r = keys_in(i + t)
                                for q in range(QT):
                                    last = nc.tensor.transpose(psb[0:r, bank, t * S + q * P:t * S + (q + 1) * P],
                                                               bias[:, q, (i + t) * P:(i + t) * P + r], w["ident16"][:, :])
                        last.then_inc(filled, 1)

                batch(0)
                with nc.tensor.Fori(1, B) as b:
                    batch(b)


def attend(nc, w, kparts_d, qparts_d, values_d, bias_d, biasT_d, heads_d):
    with ExitStack() as es:
        def sb(name, shape, dt=F32):
            return es.enter_context(nc.sbuf_tensor(name, shape, dt))

        def sem(name):
            return es.enter_context(nc.semaphore(name))

        kst = [sb(f"kst{g}", [P, HG, SK], BF16) for g in range(NG)]
        qst = [sb(f"qst{g}", [P, HG, S], BF16) for g in range(NG)]
        vst = [sb(f"vst{g}", [P, KT, HG * 2 * DH]) for g in range(NG)]
        bias, biasT = sb("bias2", [P, QT, SK], BF16), sb("biasT2", [P, KT, S], BF16)
        PR = 3
        probs = sb("probs", [P, PR, HG, S])
        outs = sb("outs", [P, 2, S])
        junk = sb("junk", [P, 2, CW], BF16)
        cmax = sb("cmax", [P, QT * HG, NCH])
        negmax, rest = sb("negmax", [P, QT * HG]), sb("rest", [P, 2, QT * HG])
        mparts, mrows = sb("mparts", [P, P // (QT * HG), QT * HG], BF16), sb("mrows", [PARTS * QT * HG, P], BF16)
        ps_s = es.enter_context(nc.psum_tensor("ps_s", [P, 2, 2, S], F32))
        ps_m = es.enter_context(nc.psum_tensor("ps_m", [P, 2, S], F32))
        ps_o = es.enter_context(nc.psum_tensor("ps_o", [P, S], F32))
        ps_t = es.enter_context(nc.psum_tensor("ps_t", [P, 1024], BF16))

        stack_init, mparts_init, wait_carrier = sem("stack_init"), sem("mparts_init"), sem("wait_carrier")
        stack_in = [sem(f"stack_in{g}") for g in range(NG)]
        bias_in = [sem(f"bias_in{t}") for t in range(QT)]
        biasT_in = sem("biasT_in")
        scored, expd, summed, out_kept = sem("scored"), sem("expd"), sem("summed"), sem("out_kept")
        out_stored = [sem("out_stored0"), sem("out_stored1")]
        max_scored, max_taken = sem("max_scored"), sem("max_taken")
        max_step, max_parts, max_tr, max_rows, max_in = sem("max_step"), sem("max_parts"), sem("max_tr"), sem("max_rows"), sem("max_in")
        NDMA = 2 * len(STACK) - 2 + 1
        PAIRS, MC = KT * 2, HG * QT * NCH
        STEPS = 6

        def load_stack(eng, g, gi):
            def rows(t, r0, r1):
                return t[r0:r1, :, :].rearrange("p h c -> p (h c)")

            kd, qd = kparts_d[gi, :, :, :, :].rearrange("a d h c -> (a d) (h c)"), qparts_d[gi, :, :, :, :].rearrange("a d h c -> (a d) (h c)")
            for dst, r0, r1, src, s0 in ((kst[g], 0, 16, kd, 0), (kst[g], 32, 64, kd, DH), (kst[g], 64, 96, kd, 0), (kst[g], 96, 112, kd, 0),
                                         (qst[g], 0, 16, qd, 0), (qst[g], 32, 48, qd, 0), (qst[g], 48, 64, qd, 0),
                                         (qst[g], 64, 80, qd, DH), (qst[g], 80, 96, qd, DH), (qst[g], 96, 112, qd, 2 * DH)):
                eng.dma_start(rows(dst, r0, r1), src[s0:s0 + r1 - r0, :]).then_inc(stack_in[g], 16)
            eng.dma_start(vst[g][:, :, :], values_d[gi, :, :, :]).then_inc(stack_in[g], 16)

        def max_rows_in(sp, g, gi):
            sp.wait_ge(max_rows, gi + 1)
            for p in range(PARTS):
                sp.dma_start(qst[g][MAX_ROW + p:MAX_ROW + p + 1, :, :].rearrange("p h c -> p (h c)"),
                             mrows[p * QT * HG:(p + 1) * QT * HG, :]).then_inc(max_in, 16)

        with nc.Block() as block:
            @block.sync
            def _(sp):
                sp.wait_ge(stack_init, 2 * NG)
                for g in range(NG):
                    load_stack(sp, g, g)
                max_rows_in(sp, 0, 0)

                def batch(b, last):
                    for g in range(NG):
                        if not (last and g == NG - 1):
                            max_rows_in(sp, (g + 1) % NG, b * NG + g + 1)
                        if not last:
                            sp.wait_ge(summed, (b * NG + g + 1) * KT)
                            load_stack(sp, g, b * NG + g + NG)

                batch(0, False)
                with nc.sync.Fori(1, B - 1) as b:
                    batch(b, False)
                batch(B - 1, True)

            @block.gpsimd
            def _(pool):
                for qt in range(QT):
                    pool.dma_start(bias[:, qt, :], bias_d[0, :, qt, :]).then_inc(bias_in[qt], 16)
                pool.dma_start(biasT[:, :, :], biasT_d[0, :, :, :]).then_inc(biasT_in, 16)
                for g in range(NG):
                    nc.gpsimd.memset(kst[g][:, :, :], 1.0).then_inc(stack_init, 1)
                    nc.gpsimd.memset(qst[g][:, :, :], 0.0).then_inc(stack_init, 1)

                def batch(b, last):
                    for g in range(NG):
                        if not last and g == NG - 2:
                            for qt in range(QT):
                                pool.wait_ge(max_taken, (b * NG + NG - 1) * MC + (qt + 1) * HG * NCH)
                                pool.dma_start(bias[:, qt, :], bias_d[b + 1, :, qt, :]).then_inc(bias_in[qt], 16)
                        pool.wait_ge(out_kept, b * NG + g + 1)
                        pool.dma_start(heads_d[b * NG + g, :, :], outs[:, g % 2, :]).then_inc(out_stored[g % 2], 16)
                    if not last:
                        pool.wait_ge(scored, (b + 1) * NG * PAIRS)
                        pool.dma_start(biasT[:, :, :], biasT_d[b + 1, :, :, :]).then_inc(biasT_in, 16)

                batch(0, False)
                with nc.gpsimd.Fori(1, B - 1) as b:
                    batch(b, False)
                batch(B - 1, True)
                for stored in out_stored:
                    pool.wait_ge(stored, B * NG // 2 * 16)

            @block.scalar
            def _(act):
                def batch(b):
                    for g in range(NG):
                        for u in range(PAIRS):
                            n, kt, half = g * PAIRS + u, u // 2, u % 2
                            tile = g * KT + kt
                            r = keys_in(kt)
                            act.wait_ge(scored, b * NG * PAIRS + n + 1)
                            if half == 0:
                                act.wait_ge(summed, b * NG * KT + max(tile - PR + 1, 0))
                            nc.scalar.activation(probs[0:r, tile % PR, 2 * half:2 * half + 2, :], ps_s[0:r, n % 2, :, :],
                                                 ACT.Exp, scale=SCALE).then_inc(expd, 1)

                batch(0)
                with nc.scalar.Fori(1, B) as b:
                    batch(b)

            @block.vector
            def _(v):
                def take_max(qt, g, m, m_all):
                    v.wait_ge(max_scored, m_all + 1)
                    v.sem_inc(wait_carrier, 1)
                    h, c = (m // NCH) % HG, m % NCH
                    c0, cn = CHUNKS[c]
                    nc.vector.tensor_tensor_reduce(junk[:, m % 2, 0:cn], ps_m[:, m % 2, 0:cn], bias[:, qt, c0:c0 + cn], 1.0, LOWEST,
                                                   ALU.add, ALU.max, cmax[:, h * QT + qt, c:c + 1]).then_inc(max_taken, 1)

                def split_max(gi):
                    base = gi * STEPS
                    v.wait_ge(max_taken, (gi + 1) * MC)
                    nc.vector.tensor_reduce(negmax[:, :], cmax[:, :, :], AX_X, ALU.max, negate=True).then_inc(max_step, 1)
                    v.wait_ge(max_step, base + 1)
                    v.wait_ge(max_tr, gi)
                    nc.vector.tensor_copy(mparts[:, 0, :], negmax[:, :]).then_inc(max_step, 1)
                    v.wait_ge(max_step, base + 2)
                    nc.vector.tensor_tensor(rest[:, 0, :], negmax[:, :], mparts[:, 0, :], ALU.subtract).then_inc(max_step, 1)
                    v.wait_ge(max_step, base + 3)
                    nc.vector.tensor_copy(mparts[:, 1, :], rest[:, 0, :]).then_inc(max_step, 1)
                    v.wait_ge(max_step, base + 4)
                    nc.vector.tensor_tensor(rest[:, 1, :], rest[:, 0, :], mparts[:, 1, :], ALU.subtract).then_inc(max_step, 1)
                    v.wait_ge(max_step, base + 5)
                    nc.vector.tensor_copy(mparts[:, 2, :], rest[:, 1, :]).then_inc(max_step, 1)
                    v.wait_ge(max_step, base + 6)
                    v.sem_inc(max_parts, 1)
                    v.wait_ge(max_tr, gi + 1)
                    v.wait_ge(max_in, gi * PARTS * 16)
                    nc.vector.tensor_copy(mrows[:, :], ps_t[0:PARTS * QT * HG, 0:P]).then_inc(max_rows, 1)

                def maxima(gi, bi, part):
                    for m in part:
                        qt = m // (HG * NCH)
                        if m % (HG * NCH) == 0:
                            v.wait_ge(bias_in[qt], bi * 16 + 16)
                        take_max(qt, 0, m, gi * MC + m)

                def keep_output(b, g, gi):
                    v.wait_ge(summed, (gi + 1) * KT)
                    v.wait_ge(out_stored[g % 2], (b * (NG // 2) + g // 2) * 16)
                    nc.vector.tensor_copy(outs[:, g % 2, :], ps_o[:, :]).then_inc(out_kept, 1)

                nc.vector.memset(mparts[:, :, :], 0.0).then_inc(mparts_init, 1)
                v.wait_ge(mparts_init, 1)
                maxima(0, 0, range(MC))
                split_max(0)

                def batch(b, last):
                    for g in range(NG):
                        gi = b * NG + g
                        nxt = not (last and g == NG - 1)
                        bi = b + 1 if g == NG - 1 else b
                        if nxt:
                            maxima(gi + 1, bi, range(0, MC // 8))
                        if g > 0:
                            keep_output(b, g - 1, gi - 1)
                        if nxt:
                            maxima(gi + 1, bi, range(MC // 8, MC))
                            split_max(gi + 1)
                        if g == NG - 1:
                            keep_output(b, g, gi)

                batch(0, False)
                with nc.vector.Fori(1, B - 1) as b:
                    batch(b, False)
                batch(B - 1, True)

            @block.tensor
            def _(pe):
                def score_for_max(g, m, m_all, fixed):
                    if not (fixed and m < 2):
                        pe.wait_ge(max_taken, m_all - 1)
                    qt, h, c = m // (HG * NCH), (m // NCH) % HG, m % NCH
                    c0, cn = CHUNKS[c]
                    nc.tensor.matmul(ps_m[:, m % 2, 0:cn], qst[g][0:MAX_ROW, h, qt * P:(qt + 1) * P],
                                     kst[g][0:MAX_ROW, h, c0:c0 + cn], start=True, stop=True).then_inc(max_scored, 1)

                def transpose_max(gi):
                    pe.wait_ge(max_parts, gi + 1)
                    pe.wait_ge(max_rows, gi)
                    nc.tensor.transpose(ps_t[:, 0:P], mparts[:, :, :].rearrange("p a n -> p (a n)"),
                                        w["ident16"][:, :]).then_inc(max_tr, 1)

                def score_pair(b, g, u):
                    n, kt, half = g * PAIRS + u, u // 2, u % 2
                    r = keys_in(kt)
                    pe.wait_ge(expd, b * NG * PAIRS + max(n - 1, 0))
                    for j in range(2):
                        h = 2 * half + j
                        nc.tensor.matmul(ps_s[0:r, n % 2, j, :], kst[g][:, h, kt * P:kt * P + r], qst[g][:, h, :],
                                         start=True, stop=False)
                    for j in range(2):
                        last = nc.tensor.matmul(ps_s[0:r, n % 2, j, :], w["ident16"][0:r, 0:r], biasT[0:r, kt, :],
                                                start=False, stop=True)
                    last.then_inc(scored, 1)

                def sum_tile(b, g, kt):
                    tile = g * KT + kt
                    r = keys_in(kt)
                    pe.wait_ge(expd, b * NG * PAIRS + 2 * tile + 2)
                    if kt == 0:
                        pe.wait_ge(out_kept, b * NG + g)
                    for h in range(HG):
                        strip = slice(2 * DH * h, 2 * DH * (h + 1))
                        last = nc.tensor.matmul(ps_o[strip, :], vst[g][0:r, kt, strip], probs[0:r, tile % PR, h, :],
                                                start=kt == 0, stop=kt == KT - 1)
                    last.then_inc(summed, 1)

                pe.wait_ge(stack_in[0], NDMA * 16)
                for m in range(MC):
                    score_for_max(0, m, m, True)
                transpose_max(0)

                def batch(b, last):
                    for g in range(NG):
                        gi = b * NG + g
                        nxt = not (last and g == NG - 1)
                        if g == 0:
                            pe.wait_ge(biasT_in, b * 16 + 16)
                        pe.wait_ge(max_in, (gi + 1) * PARTS * 16)
                        if nxt:
                            pe.wait_ge(stack_in[(g + 1) % NG], ((b + 1 if g == NG - 1 else b) + 1) * NDMA * 16)
                        done = 0
                        for u in range(PAIRS):
                            score_pair(b, g, u)
                            upto = min(MC, -(-(u + 1) * MC // (PAIRS - 2)))
                            while nxt and done < upto:
                                score_for_max((g + 1) % NG, done, (gi + 1) * MC + done, False)
                                done += 1
                            if u % 2 == 1:
                                if u > 1:
                                    sum_tile(b, g, u // 2 - 1)
                                elif g > 0:
                                    sum_tile(b, g - 1, KT - 1)
                        if nxt:
                            transpose_max(gi + 1)
                    sum_tile(b, NG - 1, KT - 1)

                batch(0, False)
                with nc.tensor.Fori(1, B - 1) as b:
                    batch(b, False)
                batch(B - 1, True)


def finish(nc, w, x, g_attn, g_ffn, wo, bo, b1, b2, heads_d, x1_d, xn_d, out):
    with ExitStack() as es:
        def sb(name, shape, dt=F32):
            return es.enter_context(nc.sbuf_tensor(name, shape, dt))

        def sem(name):
            return es.enter_context(nc.semaphore(name))

        wo_s, bo_s, gate = sb("wo_s", [P, NG, D]), sb("bo_s", [P, D]), sb("gate", [P, 2])
        b1_s, b2_s = sb("b1_s", [P, FC]), sb("b2_s", [P, D])
        sel = sb("sel", [P, HG, 2, DH])
        heads, recip, scaled = sb("heads", [P, 2, NG, S]), sb("recip", [P, NG, S]), sb("scaled", [P, NG, S])
        x_s, xb, x1 = sb("x3", [P, 2, QT, D]), sb("xb3", [P, QT, D]), sb("x1", [P, 2, QT, D])
        xn = sb("xn3", [P, 2, QT, D])
        stats, mean_var, rstd = sb("stats3", [P, QT, 6]), sb("mean_var3", [P, QT, 2]), sb("rstd3", [P, QT, 2])
        ps = es.enter_context(nc.psum_tensor("ps3", [P, 8, 512], F32))

        consts_in, gates_ready, prep, sel_step, sel_ready = sem("consts_in"), sem("gates_ready"), sem("prep"), sem("sel_step"), sem("sel_ready")
        heads_in, x_in = [sem("heads_in0"), sem("heads_in1")], [sem("x_in0"), sem("x_in1")]
        spread, rec_ready, scaled_ready, projected = sem("spread"), sem("rec_ready"), sem("scaled_ready"), sem("projected")
        xb_ready, x1_ready, ln_step, var_ready, std_ready, xn_ready = sem("xb_ready"), sem("x1_ready"), sem("ln_step3"), sem("var_ready3"), sem("std_ready3"), sem("xn_ready3")
        x1_out = [sem("x1_out0"), sem("x1_out1")]

        with nc.Block() as block:
            @block.sync
            def _(sp):
                sp.wait_ge(sel_step, 1)
                for g in range(NG):
                    for h in range(HG):
                        r0 = (g * HG + h) * DH
                        sp.dma_start(wo_s[2 * DH * h:2 * DH * h + DH, g, :], wo[r0:r0 + DH, :]).then_inc(consts_in, 16)
                sp.dma_start(bo_s[:, :], bo.rearrange("(a d) -> a d", a=1).to_broadcast([P, D])).then_inc(consts_in, 16)
                sp.dma_start(b2_s[:, :], b2.rearrange("(a d) -> a d", a=1).to_broadcast([P, D])).then_inc(consts_in, 16)
                sp.dma_start(gate[:, 0:1], g_attn.rearrange("(a d) -> a d", a=1).to_broadcast([P, 1])).then_inc(consts_in, 16)
                sp.dma_start(gate[:, 1:2], g_ffn.rearrange("(a d) -> a d", a=1).to_broadcast([P, 1])).then_inc(consts_in, 16)
                for b in range(B):
                    if b >= 2:
                        sp.wait_ge(scaled_ready, (b - 1) * NG)
                        sp.wait_ge(xb_ready, b - 1)
                    sp.dma_start(heads[:, b % 2, :, :], heads_d[b * NG:(b + 1) * NG, :, :].rearrange("g p c -> p g c")).then_inc(heads_in[b % 2], 16)
                    sp.dma_start(x_s[:, b % 2, :, :], x[b, :, :].rearrange("(t p) d -> p t d", p=P)).then_inc(x_in[b % 2], 16)

            @block.gpsimd
            def _(pool):
                nc.gpsimd.memset(wo_s[:, :, :], 0.0).then_inc(sel_step, 1)
                nc.gpsimd.memset(sel[:, :, :, :], 0.0).then_inc(sel_step, 1)
                pool.wait_ge(sel_step, 2)
                nc.gpsimd.affine_select(out=sel[:, :, :, :].rearrange("p h a d -> p h (a d)"), in_=sel[:, :, :, :].rearrange("p h a d -> p h (a d)"),
                                        compare_op=ALU.not_equal, fill=1.0, base=-DH, pattern=[[-2 * DH, HG], [0, 2 * DH]],
                                        channel_multiplier=1).then_inc(sel_ready, 1)
                pool.wait_ge(gates_ready, 1)
                nc.gpsimd.tensor_scalar(bo_s[:, :], bo_s[:, :], gate[:, 0:1], None, ALU.mult).then_inc(prep, 1)
                for b in range(B):
                    pool.wait_ge(x_in[b % 2], 16 * (b // 2) + 16)
                    pool.wait_ge(prep, 1)
                    if b:
                        pool.wait_ge(x1_ready, b * QT)
                    for t in range(QT):
                        last = nc.gpsimd.tensor_tensor(xb[:, t, :], x_s[:, b % 2, t, :], bo_s[:, :], ALU.add)
                    last.then_inc(xb_ready, 1)
                    pool.wait_ge(xn_ready, (b + 1) * QT)
                    pool.dma_start(x1_d[b, :, :, :], x1[:, b % 2, :, :]).then_inc(x1_out[b % 2], 16)
                    pool.dma_start(xn_d[b, :, :, :], xn[:, b % 2, :, :]).then_inc(x1_out[b % 2], 16)
                for stored in x1_out:
                    pool.wait_ge(stored, B // 2 * 32)

            @block.scalar
            def _(act):
                act.wait_ge(consts_in, (NG * HG + 4) * 16)
                nc.scalar.activation(gate[:, :], gate[:, :], ACT.Tanh).then_inc(gates_ready, 1)
                for b in range(B):
                    act.wait_ge(var_ready, b + 1)
                    nc.scalar.activation(rstd[:, :, 0], rstd[:, :, 0], ACT.Sqrt).then_inc(std_ready, 1)

            @block.vector
            def _(v):
                v.wait_ge(gates_ready, 1)

                def project_add(b):
                    v.wait_ge(xb_ready, b + 1)
                    if b >= 2:
                        v.wait_ge(x1_out[b % 2], b // 2 * 32)
                    for t in range(QT):
                        v.wait_ge(projected, b * QT + t + 1)
                        nc.vector.scalar_tensor_tensor(x1[:, b % 2, t, :], ps[:, 4 + t, 0:D], gate[:, 0:1], xb[:, t, :],
                                                       ALU.mult, ALU.add).then_inc(x1_ready, 1)
                    base = b * (2 * QT + 1)
                    v.wait_ge(x1_ready, (b + 1) * QT)
                    for t in range(QT):
                        nc.vector.bn_stats(stats[:, t, :], x1[:, b % 2, t, :]).then_inc(ln_step, 1)
                    v.wait_ge(ln_step, base + QT)
                    for t in range(QT):
                        nc.vector.bn_aggr(mean_var[:, t, :], stats[:, t, :]).then_inc(ln_step, 1)
                    v.wait_ge(ln_step, base + 2 * QT)
                    layernorm_scales(nc, v, mean_var, rstd, var_ready, std_ready, ln_step, base + 2 * QT + 1, b)
                    for t in range(QT):
                        nc.vector.tensor_scalar(xn[:, b % 2, t, :], x1[:, b % 2, t, :], mean_var[:, t, 0:1], rstd[:, t, 1:2],
                                                ALU.subtract, ALU.mult).then_inc(xn_ready, 1)

                for b in range(B):
                    for g in range(NG):
                        v.wait_ge(spread, b * NG + g + 1)
                        nc.vector.reciprocal(recip[:, g, :], ps[:, g, :]).then_inc(rec_ready, 1)
                        v.wait_ge(rec_ready, b * NG + g + 1)
                        if b and g == 0:
                            v.wait_ge(projected, b * QT)
                        nc.vector.tensor_tensor(scaled[:, g, :], heads[:, b % 2, g, :], recip[:, g, :], ALU.mult).then_inc(scaled_ready, 1)
                    project_add(b)

            @block.tensor
            def _(pe):
                pe.wait_ge(sel_ready, 1)
                pe.wait_ge(consts_in, (NG * HG + 4) * 16)
                for b in range(B):
                    pe.wait_ge(heads_in[b % 2], 16 * (b // 2) + 16)
                    if b:
                        pe.wait_ge(rec_ready, b * NG)
                    for g in range(NG):
                        nc.tensor.matmul(ps[:, g, :], sel[:, :, :, :].rearrange("p h a d -> p (h a d)"), heads[:, b % 2, g, :],
                                         start=True, stop=True).then_inc(spread, 1)
                    pe.wait_ge(scaled_ready, (b + 1) * NG)
                    if b:
                        pe.wait_ge(x1_ready, b * QT)
                    for t in range(QT):
                        for g in range(NG):
                            last = nc.tensor.matmul(ps[:, 4 + t, 0:D], scaled[:, g, t * P:(t + 1) * P], wo_s[:, g, :],
                                                    start=g == 0, stop=g == NG - 1)
                        last.then_inc(projected, 1)

    with ExitStack() as es:
        def sb(name, shape, dt=F32):
            return es.enter_context(nc.sbuf_tensor(name, shape, dt))

        def sem(name):
            return es.enter_context(nc.semaphore(name))

        b1_s, b2_s, gate = sb("b1_f", [P, FC]), sb("b2_f", [P, D]), sb("gate_f", [P, 1])
        x1, xn = sb("x1_f", [P, 2, QT, D]), sb("xn_f", [P, 2, QT, D])
        xT, hT = sb("xT_f", [P, 2, DC, S]), sb("hT_f", [P, 2, FC, S])
        xb, y = sb("xb_f", [P, 2, QT, D]), sb("y_f", [P, 2, QT, D])
        ps_t = es.enter_context(nc.psum_tensor("ps_xt", [P, 2, S], F32))
        ps_h = es.enter_context(nc.psum_tensor("ps_h", [P, 4, S], F32))
        ps_y = es.enter_context(nc.psum_tensor("ps_y", [P, 2, S], F32))
        consts_in, gate_ready, prep = sem("consts_in_f"), sem("gate_ready_f"), sem("prep_f")
        rows_in = [sem("rows_in0"), sem("rows_in1")]
        transposed, xT_ready, hidden, gelu_ready, summed, y_ready, y_out, xb_ready = (
            sem("transposed_f"), sem("xT_ready_f"), sem("hidden_f"), sem("gelu_ready_f"), sem("summed_f"), sem("y_ready_f"), [sem("y_out0"), sem("y_out1")], sem("xb_ready_f"))

        with nc.Block() as block:
            @block.sync
            def _(sp):
                sp.dma_start(gate[:, :], g_ffn.rearrange("(a d) -> a d", a=1).to_broadcast([P, 1])).then_inc(consts_in, 16)
                sp.dma_start(b2_s[:, :], b2.rearrange("(a d) -> a d", a=1).to_broadcast([P, D])).then_inc(consts_in, 16)
                sp.dma_start(b1_s[:, :], b1.rearrange("(c p) -> p c", p=P), allow_slow_non_contiguous=True).then_inc(consts_in, 16)
                for b in range(B):
                    if b >= 2:
                        sp.wait_ge(transposed, (b - 1) * DC)
                        sp.wait_ge(xb_ready, b - 1)
                    sp.dma_start(xn[:, b % 2, :, :], xn_d[b, :, :, :]).then_inc(rows_in[b % 2], 16)
                    sp.dma_start(x1[:, b % 2, :, :], x1_d[b, :, :, :]).then_inc(rows_in[b % 2], 16)

            @block.gpsimd
            def _(pool):
                pool.wait_ge(gate_ready, 1)
                nc.gpsimd.tensor_scalar(b2_s[:, :], b2_s[:, :], gate[:, 0:1], None, ALU.mult).then_inc(prep, 1)
                pool.wait_ge(prep, 1)
                for b in range(B):
                    pool.wait_ge(rows_in[b % 2], 32 * (b // 2) + 32)
                    if b >= 2:
                        pool.wait_ge(y_ready, (b - 1) * QT)
                    for t in range(QT):
                        last = nc.gpsimd.tensor_tensor(xb[:, b % 2, t, :], x1[:, b % 2, t, :], b2_s[:, :], ALU.add)
                    last.then_inc(xb_ready, 1)
                    if b >= 1:
                        pool.wait_ge(y_ready, b * QT)
                        pool.dma_start(out[b - 1, :, :].rearrange("(t p) d -> p t d", p=P), y[:, (b - 1) % 2, :, :]).then_inc(y_out[(b - 1) % 2], 16)
                pool.wait_ge(y_ready, B * QT)
                pool.dma_start(out[B - 1, :, :].rearrange("(t p) d -> p t d", p=P), y[:, (B - 1) % 2, :, :]).then_inc(y_out[(B - 1) % 2], 16)
                for stored in y_out:
                    pool.wait_ge(stored, B // 2 * 16)

            @block.scalar
            def _(act):
                act.wait_ge(consts_in, 48)
                nc.scalar.activation(gate[:, :], gate[:, :], ACT.Tanh).then_inc(gate_ready, 1)
                for b in range(B):
                    if b >= 2:
                        act.wait_ge(summed, (b - 1) * QT)
                    for f in range(FC):
                        act.wait_ge(hidden, b * FC + f + 1)
                        nc.scalar.activation(hT[:, b % 2, f, :], ps_h[:, (b * FC + f) % 4, :], ACT.Gelu, bias=b1_s[:, f:f + 1]).then_inc(gelu_ready, 1)

            @block.vector
            def _(v):
                v.wait_ge(gate_ready, 1)
                def keep_xT(b):
                    if b >= 2:
                        v.wait_ge(hidden, (b - 1) * FC)
                    for c in range(DC):
                        v.wait_ge(transposed, b * DC + c + 1)
                        nc.vector.tensor_copy(xT[:, b % 2, c, :], ps_t[:, c, :]).then_inc(xT_ready, 1)

                keep_xT(0)
                for b in range(B):
                    if b + 1 < B:
                        keep_xT(b + 1)
                    v.wait_ge(xb_ready, b + 1)
                    if b >= 2:
                        v.wait_ge(y_out[b % 2], b // 2 * 16)
                    for t in range(QT):
                        v.wait_ge(summed, b * QT + t + 1)
                        nc.vector.scalar_tensor_tensor(y[:, b % 2, t, :], ps_y[:, t % 2, 0:D], gate[:, 0:1], xb[:, b % 2, t, :],
                                                       ALU.mult, ALU.add).then_inc(y_ready, 1)

            @block.tensor
            def _(pe):
                def transposes(b):
                    pe.wait_ge(rows_in[b % 2], 32 * (b // 2) + 32)
                    if b:
                        pe.wait_ge(xT_ready, b * DC)
                    for c in range(DC):
                        for t in range(QT):
                            last = nc.tensor.transpose(ps_t[:, c, t * P:(t + 1) * P], xn[:, b % 2, t, c * P:(c + 1) * P], w["ident"][:, :])
                        last.then_inc(transposed, 1)

                def second(b):
                    pe.wait_ge(gelu_ready, (b + 1) * FC)
                    for t in range(QT):
                        if b * QT + t >= 2:
                            pe.wait_ge(y_ready, b * QT + t - 1)
                        for f in range(FC):
                            last = nc.tensor.matmul(ps_y[:, t % 2, 0:D], hT[:, b % 2, f, t * P:(t + 1) * P], w["w2T"][:, f, :],
                                                    start=f == 0, stop=f == FC - 1)
                        last.then_inc(summed, 1)

                transposes(0)
                for b in range(B):
                    if b + 1 < B:
                        transposes(b + 1)
                    pe.wait_ge(xT_ready, (b + 1) * DC)
                    for f in range(FC):
                        if b * FC + f >= 4:
                            pe.wait_ge(gelu_ready, b * FC + f - 3)
                        for c in range(DC):
                            last = nc.tensor.matmul(ps_h[:, (b * FC + f) % 4, :], w["w1T"][:, c, f * P:(f + 1) * P], xT[:, b % 2, c, :],
                                                    start=c == 0, stop=c == DC - 1)
                        last.then_inc(hidden, 1)
                    if b >= 1:
                        second(b - 1)
                second(B - 1)


def gated_cross_attention_block(nc, x, ctx_in, mask, g_attn, g_ffn, wq, bq, wk, bk, wv, bv, wo, bo, w1, b1, w2, b2, out):
    def dram(name, shape, dt=F32):
        return nc.dram_tensor(name, shape, dt, kind="Internal").ap()

    kparts_d = dram("kparts_d", (B * NG, PARTS, DH, HG, SK), BF16)
    qparts_d = dram("qparts_d", (B * NG, PARTS, DH, HG, S), BF16)
    values_d = dram("values_d", (B * NG, P, KT, HG * 2 * DH))
    bias_d = dram("bias_d", (B, P, QT, SK), BF16)
    biasT_d = dram("biasT_d", (B, P, KT, S), BF16)
    heads_d = dram("heads_d", (B * NG, P, S))
    x1_d, xn_d = dram("x1_d", (B, P, QT, D)), dram("xn_d", (B, P, QT, D))
    with ExitStack() as es:
        w = {
            "ident": es.enter_context(nc.sbuf_tensor("ident", [P, P], F32)),
            "ident16": es.enter_context(nc.sbuf_tensor("ident16", [P, P], BF16)),
            "w1T": es.enter_context(nc.sbuf_tensor("w1T", [P, DC, F], F32)),
            "w2T": es.enter_context(nc.sbuf_tensor("w2T", [P, FC, D], F32)),
        }
        prepare(nc, w, x, ctx_in, mask, wq, bq, wk, bk, wv, bv, w1, w2, kparts_d, qparts_d, values_d, bias_d, biasT_d)
        attend(nc, w, kparts_d, qparts_d, values_d, bias_d, biasT_d, heads_d)
        finish(nc, w, x, g_attn, g_ffn, wo, bo, b1, b2, heads_d, x1_d, xn_d, out)


_INS = ["x", "ctx_1024", "mask_BxSxS2_ik1", "g_xattn", "g_ffn", "L0_xattn_Wq", "L0_xattn_bq", "L0_xattn_Wk", "L0_xattn_bk",
        "L0_xattn_Wv", "L0_xattn_bv", "L0_xattn_Wo", "L0_xattn_bo", "L0_ffn_w1", "L0_ffn_b1", "L0_ffn_w2", "L0_ffn_b2"]


def kernel(**inputs):
    import numpy as _np
    import concourse.bacc as _bacc
    from concourse import mybir as _mybir
    from concourse.bass_utils import run_bass_kernel_spmd as _run

    nc = _bacc.Bacc("TRN2", target_bir_lowering=False, num_devices=1)
    arrays, args = {}, []
    for name in _INS:
        a = _np.ascontiguousarray(inputs[name])
        arrays[f"in_{name}_dram"] = a
        args.append(nc.dram_tensor(f"in_{name}_dram", a.shape, _mybir.dt.from_np(a.dtype), kind="ExternalInput").ap())
    args.append(nc.dram_tensor("out_0_dram", (B, S, D), F32, kind="ExternalOutput").ap())
    gated_cross_attention_block(nc, *args)
    r = _run(nc, [arrays], core_ids=[0])
    return r.results[0]["out_0_dram"]
```

```python
from contextlib import ExitStack

import concourse.bass as bass
from concourse import mybir

ALU = mybir.AluOpType
ACT = mybir.ActivationFunctionType
AX_X = mybir.AxisListType.X
F32 = mybir.dt.float32
BF16 = mybir.dt.bfloat16
I32 = mybir.dt.int32

P = 128
B, S, D = 4, 512, 256
SK = 1601
H, DH = 16, 16
F = 1024
DC = D // P
QT = S // P
FC = F // P
KT = -(-SK // P)
KLAST = SK - (KT - 1) * P
HG = 4
NG = H // HG
GR = HG * DH
PARTS = 3
SCALE = float(DH) ** -0.5
MASKED = -(2.0 ** 100)
LOWEST = -3.0e38
LN_EPS = 1e-5

STACK = [(0, 0, 0), (32, 0, 1), (48, 0, 2), (64, 1, 0), (80, 1, 1), (96, 2, 0)]
MASK_ROW = 16
MAX_ROW = 112

KEY_BLOCKS = [(k, min(512, SK - k)) for k in range(0, SK, 512)]
NCH = 2
CW = -(-SK // NCH)
CHUNKS = [(c * CW, min(CW, SK - c * CW)) for c in range(NCH)]


def keys_in(kt):
    return KLAST if kt == KT - 1 else P


def layernorm_scales(nc, v, mean_var, rstd, var_ready, std_ready, step, base, index):
    nc.vector.tensor_scalar(rstd[:, :, 0], mean_var[:, :, 1], LN_EPS, None, ALU.add).then_inc(var_ready, 1)
    v.wait_ge(std_ready, index + 1)
    nc.vector.reciprocal(rstd[:, :, 1], rstd[:, :, 0]).then_inc(step, 1)
    v.wait_ge(step, base)


def prepare(nc, w, x, ctx_in, mask, wq, bq, wk, bk, wv, bv, w1, w2, kparts_d, qparts_d, values_d, bias_d, biasT_d,
            maskrow_d, ones_d, zeros_d):
    with ExitStack() as es:
        def sb(name, shape, dt=F32):
            return es.enter_context(nc.sbuf_tensor(name, shape, dt))

        def sem(name):
            return es.enter_context(nc.semaphore(name))

        wq_s, wk_s, wv_s = sb("wq_s", [P, DC, D]), sb("wk_s", [P, DC, D]), sb("wv_s", [P, DC, D])
        bq_s, bk_s, bv_s = sb("bq_s", [P, DC]), sb("bk_s", [P, DC]), sb("bv_s", [P, D])
        x_s, xn, xT = sb("x_s", [P, QT, D]), sb("xn", [P, QT, D]), sb("xT", [P, DC, S])
        stats, mean_var, rstd = sb("stats", [P, QT, 6]), sb("mean_var", [P, QT, 2]), sb("rstd", [P, QT, 2])
        c_s, cT = sb("c_s", [P, KT, D]), sb("cT", [P, DC, SK])
        kp, krest = sb("kp", [P, PARTS, DC, SK], BF16), sb("krest", [P, DC, SK])
        qp, qrest = sb("qp", [P, PARTS, DC, S], BF16), sb("qrest", [P, DC, S])
        vals = sb("vals", [P, KT, H, 2 * DH])
        m_s, bias, biasT = sb("m_s", [P, 2, SK], I32), sb("bias", [P, QT, SK], BF16), sb("biasT", [P, KT, S], BF16)
        w1_s = cT[:, :, :].rearrange("p a b -> p (a b)")[:, 0:FC * D].rearrange("p (c d) -> p c d", c=FC)
        w2_s = krest[:, :, :].rearrange("p a b -> p (a b)")[:, 0:DC * F].rearrange("p (c d) -> p c d", c=DC)
        a1, a2 = sb("a1", [P, FC]), sb("a2", [P, DC])
        ones16 = sb("ones16", [P, 2], BF16)
        masksum, maskodd, maskrow = sb("masksum", [1, SK]), sb("maskodd", [1, SK]), sb("maskrow", [1, SK], BF16)
        same = sb("same", [1, 2])
        fill = sb("fill", [DH, SK + S], BF16)
        ps = es.enter_context(nc.psum_tensor("ps1", [P, 8, 512], F32))
        psb = ps[:, :, :].bitcast(BF16)

        weights_in, ffn_in = sem("weights_in"), sem("ffn_in")
        ident_step, consts_ready = sem("ident_step"), sem("consts_ready")
        alpha_sum, alpha_ready, sign_ready = sem("alpha_sum"), sem("alpha_ready"), sem("sign_ready")
        ffn_scaled, ffn_tr, ffn_kept = sem("ffn_scaled"), sem("ffn_tr"), sem("ffn_kept")
        x_in, c_in, m_in = sem("x_in"), sem("c_in"), [sem("m_in0"), sem("m_in1")]
        ln_step, var_ready, std_ready, xn_ready = sem("ln_step"), sem("var_ready"), sem("std_ready"), sem("xn_ready")
        filled, act_freed, dve_freed = sem("filled"), sem("act_freed"), sem("dve_freed")
        hi_ready, rest_ready, mid_ready, lo_ready = sem("hi_ready"), sem("rest_ready"), sem("mid_ready"), sem("lo_ready")
        bias_ready, wait_carrier = sem("bias_ready"), sem("wait_carrier1")
        row_step, row_out, fill_out = sem("row_step"), sem("row_out"), sem("fill_out")
        qk_out, v_out, bias_out, biasT_out = sem("qk_out"), sem("v_out"), sem("bias_out"), sem("biasT_out")

        jobs = [("cT", c, kb) for kb in range(len(KEY_BLOCKS)) for c in range(DC)]
        jobs += [("xT", c, 0) for c in range(DC)]
        jobs += [("q", m, 0) for m in range(DC)]
        jobs += [("k", m, kb) for m in range(DC) for kb in range(len(KEY_BLOCKS))]
        pairs = list(range(0, KT, 2))
        for kt in pairs:
            jobs += [("v", kt, 0), ("m", kt, 0)]
            if kt // 2 >= 1 and kt // 2 <= len(KEY_BLOCKS):
                jobs += [("sum", 0, kt // 2 - 1)]
        jobs_act = [j for j in jobs if j[0] in ("cT", "xT", "m", "sum")]
        jobs_dve = [j for j in jobs if j[0] in ("q", "k", "v")]
        splits = [j for j in jobs if j[0] in ("q", "k")]
        NJ, NA, NV, NS = len(jobs), len(jobs_act), len(jobs_dve), len(splits)
        ROW_STEPS = 6

        def job_done(b, job):
            return b * NJ + jobs.index(job) + 1

        def bank_before(n):
            if n >= 8:
                return jobs[n - 8], False
            return [j for k, j in enumerate(jobs) if k % 8 == n][-1], True

        def first(b):
            return type(b) is int and b == 0

        def operand(kind, m, kb):
            if kind == "q":
                return qp, qrest, bq_s, m, 0, S
            return kp, krest, bk_s, m, KEY_BLOCKS[kb][0], KEY_BLOCKS[kb][1]

        with nc.Block() as block:
            @block.sync
            def _(sp):
                sp.dma_start(w1_s, w1.rearrange("(c p) d -> p c d", p=P)).then_inc(ffn_in, 16)
                sp.dma_start(w2_s, w2.rearrange("(c p) d -> p c d", p=P)).then_inc(ffn_in, 16)
                for dst, src in ((wq_s, wq), (wk_s, wk), (wv_s, wv)):
                    sp.dma_start(dst[:, :, :], src.rearrange("(c p) d -> p c d", p=P)).then_inc(weights_in, 16)
                for dst, src in ((bq_s, bq), (bk_s, bk)):
                    sp.dma_start(dst[:, :], src.rearrange("(c p) -> p c", p=P), allow_slow_non_contiguous=True).then_inc(weights_in, 16)
                sp.dma_start(bv_s[:, :], bv.rearrange("(a d) -> a d", a=1).to_broadcast([P, D])).then_inc(weights_in, 16)
                sp.wait_ge(consts_ready, 6)
                for h in range(HG):
                    sp.dma_start(ones_d[:, h, :], fill[:, 0:SK]).then_inc(fill_out, 16)
                    sp.dma_start(zeros_d[:, h, :], fill[:, SK:SK + S]).then_inc(fill_out, 16)

                def load_rows(b):
                    sp.wait_ge(xn_ready, b * QT)
                    sp.dma_start(x_s[:, :, :], x[b, :, :].rearrange("(t p) d -> p t d", p=P)).then_inc(x_in, 16)
                    if not first(b):
                        sp.wait_ge(filled, b * NJ - NJ + jobs.index(("cT", DC - 1, len(KEY_BLOCKS) - 1)) + 1)
                    sp.dma_start(c_s[:, 0:KT - 1, :], ctx_in[b, 0:(KT - 1) * P, :].rearrange("(t p) d -> p t d", p=P)).then_inc(c_in, 16)
                    sp.dma_start(c_s[0:KLAST, KT - 1, :], ctx_in[b, (KT - 1) * P:SK, :]).then_inc(c_in, 16)

                def store(b):
                    sp.wait_ge(bias_ready, b * QT + QT)
                    sp.dma_start(bias_d[b, :, :, :], bias[:, :, :]).then_inc(bias_out, 16)
                    for m in range(DC):
                        sp.wait_ge(lo_ready, b * NS + splits.index(("k", m, len(KEY_BLOCKS) - 1)) + 1)
                        for g in (2 * m, 2 * m + 1):
                            rows = slice(GR * (g % 2), GR * (g % 2) + GR)
                            for part in range(PARTS):
                                sp.dma_start(kparts_d[b * NG + g, part, :, :, :].rearrange("d h c -> h d c"),
                                             kp[rows, part, m, :]).then_inc(qk_out, 16)
                                sp.dma_start(qparts_d[b * NG + g, part, :, :, :].rearrange("d h c -> h d c"),
                                             qp[rows, part, m, :]).then_inc(qk_out, 16)
                    sp.wait_ge(dve_freed, b * NV + NV)
                    for g in range(NG):
                        sp.dma_start(values_d[b * NG + g, :, :, :],
                                     vals[:, :, HG * g:HG * (g + 1), :].rearrange("p t h c -> p t (h c)")).then_inc(v_out, 16)
                    sp.wait_ge(act_freed, b * NA + NA)
                    sp.dma_start(biasT_d[b, :, :, :], biasT[:, :, :]).then_inc(biasT_out, 16)
                    sp.wait_ge(row_step, b * ROW_STEPS + ROW_STEPS)
                    sp.dma_start(maskrow_d[bass.ds(b, 1), :], maskrow[:, :]).then_inc(row_out, 16)

                load_rows(0)
                load_rows(1)
                store(0)
                with nc.sync.Fori(1, B - 1) as b:
                    load_rows(b + 1)
                    store(b)
                store(B - 1)
                sp.wait_ge(fill_out, 2 * HG * 16)
                sp.wait_ge(row_out, B * 16)
                sp.wait_ge(qk_out, B * NG * PARTS * 2 * 16)
                sp.wait_ge(v_out, B * NG * 16)
                sp.wait_ge(bias_out, B * 16)
                sp.wait_ge(biasT_out, B * 16)

            @block.gpsimd
            def _(pool):
                nc.gpsimd.memset(w["ident"][:, :], 0.0).then_inc(ident_step, 1)
                nc.gpsimd.memset(w["ident16"][:, :], 0.0).then_inc(ident_step, 1)
                nc.gpsimd.memset(vals[:, :, :, :], 1.0).then_inc(consts_ready, 1)
                nc.gpsimd.memset(biasT[:, KT - 1, :], 0.0).then_inc(consts_ready, 1)
                nc.gpsimd.memset(ones16[:, :], 1.0).then_inc(consts_ready, 1)
                nc.gpsimd.memset(fill[:, 0:SK], 1.0).then_inc(ident_step, 1)
                nc.gpsimd.memset(fill[:, SK:SK + S], 0.0).then_inc(ident_step, 1)
                pool.wait_ge(ident_step, 4)
                nc.gpsimd.memset(fill[0:1, SK:SK + S], 1.0).then_inc(consts_ready, 1)
                for m in (w["ident"], w["ident16"]):
                    nc.gpsimd.affine_select(out=m[:, :], in_=m[:, :], compare_op=ALU.not_equal, fill=1.0, base=0,
                                            pattern=[[-1, P]], channel_multiplier=1).then_inc(consts_ready, 1)
                def batch(b):
                    done = 0

                    def load_mask(qt):
                        pool.wait_ge(bias_ready, b * QT + (qt - 1 if qt >= 2 else 0))
                        pool.dma_start(m_s[:, qt % 2, :], mask[b, qt * P:(qt + 1) * P, :]).then_inc(m_in[qt % 2], 16)

                    load_mask(0)
                    load_mask(1)
                    for n, (kind, m, kb) in enumerate(splits):
                        parts, rest, _, m, c0, cn = operand(kind, m, kb)
                        pool.wait_ge(mid_ready, b * NS + n + 1)
                        nc.gpsimd.tensor_tensor(parts[:, 2, m, c0:c0 + cn], rest[:, m, c0:c0 + cn],
                                                parts[:, 1, m, c0:c0 + cn], ALU.subtract).then_inc(lo_ready, 1)
                        if n in (1, 3):
                            load_mask(2 + n // 2)

                batch(0)
                with nc.gpsimd.Fori(1, B) as b:
                    batch(b)

            @block.scalar
            def _(act):
                act.wait_ge(ffn_in, 32)
                act.wait_ge(alpha_sum, 2)
                nc.scalar.activation(w1_s, w1_s, ACT.Sign).then_inc(sign_ready, 1)
                nc.scalar.activation(w2_s, w2_s, ACT.Sign).then_inc(sign_ready, 1)
                for n in range(2 * DC * 2):
                    act.wait_ge(ffn_tr, n + 1)
                    if n < 2 * DC:
                        dst = w["w1T"][:, n // 2, (n % 2) * 512:(n % 2 + 1) * 512]
                        src = ps[:, n, :]
                    else:
                        k = n - 2 * DC
                        dst, src = w["w2T"][:, 2 * k:2 * k + 2, :], ps[:, n, :].rearrange("p (a d) -> p a d", a=2)
                    nc.scalar.activation(dst, src, ACT.Copy).then_inc(ffn_kept, 1)
                def batch(b):
                    act.wait_ge(var_ready, b + 1)
                    nc.scalar.activation(rstd[:, :, 0], rstd[:, :, 0], ACT.Sqrt).then_inc(std_ready, 1)
                    n_split = 0

                    def round_mid(n):
                        kind, m, kb = splits[n]
                        parts, rest, _, m, c0, cn = operand(kind, m, kb)
                        act.wait_ge(rest_ready, b * NS + n + 1)
                        nc.scalar.activation(parts[:, 1, m, c0:c0 + cn], rest[:, m, c0:c0 + cn], ACT.Copy).then_inc(mid_ready, 1)

                    for n, (kind, i, kb) in enumerate(jobs):
                        bank = n % 8
                        if kind == "v":
                            continue
                        act.wait_ge(filled, b * NJ + n + 1)
                        if kind == "cT":
                            k0, kn = KEY_BLOCKS[kb]
                            nc.scalar.activation(cT[:, i, k0:k0 + kn], ps[:, bank, 0:kn], ACT.Copy).then_inc(act_freed, 1)
                        elif kind == "sum":
                            if kb == 0:
                                act.wait_ge(row_step, b * ROW_STEPS)
                            k0, kn = KEY_BLOCKS[kb]
                            nc.scalar.activation(masksum[:, k0:k0 + kn], ps[0:1, bank, 0:kn], ACT.Copy, scale=1.0 / MASKED).then_inc(act_freed, 1)
                        elif kind == "xT":
                            nc.scalar.activation(xT[:, i, :], ps[:, bank, :], ACT.Copy).then_inc(act_freed, 1)
                        elif kind == "m":
                            act.wait_ge(biasT_out, b * 16)
                            if i == 0:
                                act.wait_ge(consts_ready, 6)
                            if i == KT - 1:
                                nc.scalar.activation(biasT[0:KLAST, i, :], psb[0:KLAST, bank, 0:S], ACT.Copy).then_inc(act_freed, 1)
                            else:
                                nc.scalar.activation(biasT[:, i:i + 2, :], psb[:, bank, :].rearrange("p (a s) -> p a s", a=2),
                                                     ACT.Copy).then_inc(act_freed, 1)
                        else:
                            parts, rest, bias_s, m, c0, cn = operand(kind, i, kb)
                            if n_split == 0:
                                act.wait_ge(qk_out, b * NG * PARTS * 2 * 16)
                                act.wait_ge(weights_in, 6 * 16)
                            nc.scalar.activation(parts[:, 0, m, c0:c0 + cn], ps[:, bank, 0:cn], ACT.Identity,
                                                 bias=bias_s[:, m:m + 1]).then_inc(hi_ready, 1)
                            if n_split >= 1:
                                round_mid(n_split - 1)
                            n_split += 1
                            if n_split == NS:
                                round_mid(NS - 1)

                batch(0)
                with nc.scalar.Fori(1, B) as b:
                    batch(b)

            @block.vector
            def _(v):
                v.wait_ge(ffn_in, 32)
                nc.vector.tensor_reduce(a1[:, :], w1_s, AX_X, ALU.add, apply_absolute_value=True).then_inc(alpha_sum, 1)
                nc.vector.tensor_reduce(a2[:, :], w2_s, AX_X, ALU.add, apply_absolute_value=True).then_inc(alpha_sum, 1)
                v.wait_ge(alpha_sum, 2)
                nc.vector.tensor_scalar(a1[:, :], a1[:, :], 1.0 / D, None, ALU.mult).then_inc(alpha_ready, 1)
                nc.vector.tensor_scalar(a2[:, :], a2[:, :], 1.0 / F, None, ALU.mult).then_inc(alpha_ready, 1)
                v.wait_ge(alpha_ready, 2)
                v.wait_ge(sign_ready, 2)
                for c in range(FC):
                    nc.vector.tensor_scalar(w1_s[:, c, :], w1_s[:, c, :], a1[:, c:c + 1], None, ALU.mult).then_inc(ffn_scaled, 1)
                for c in range(DC):
                    nc.vector.tensor_scalar(w2_s[:, c, :], w2_s[:, c, :], a2[:, c:c + 1], None, ALU.mult).then_inc(ffn_scaled, 1)
                v.wait_ge(weights_in, 6 * 16)
                v.wait_ge(consts_ready, 6)
                def batch(b):
                    v.wait_ge(x_in, 16 * b + 16)
                    for t in range(QT):
                        nc.vector.bn_stats(stats[:, t, :], x_s[:, t, :]).then_inc(ln_step, 1)
                    v.wait_ge(ln_step, b * (2 * QT + 1) + QT)
                    v.sem_inc(wait_carrier, 1)
                    for t in range(QT):
                        nc.vector.bn_aggr(mean_var[:, t, :], stats[:, t, :]).then_inc(ln_step, 1)
                    v.wait_ge(ln_step, b * (2 * QT + 1) + 2 * QT)
                    layernorm_scales(nc, v, mean_var, rstd, var_ready, std_ready, ln_step, b * (2 * QT + 1) + 2 * QT + 1, b)
                    if not first(b):
                        v.wait_ge(filled, b * NJ - NJ + jobs.index(("xT", DC - 1, 0)) + 1)
                    for t in range(QT):
                        nc.vector.tensor_scalar(xn[:, t, :], x_s[:, t, :], mean_var[:, t, 0:1], rstd[:, t, 1:2],
                                                ALU.subtract, ALU.mult).then_inc(xn_ready, 1)
                    v.wait_ge(bias_out, 16 * b)
                    converted = 0
                    n_split = 0
                    for n, (kind, i, kb) in enumerate(jobs):
                        bank = n % 8
                        if kind in ("q", "k"):
                            parts, rest, bias_s, m, c0, cn = operand(kind, i, kb)
                            v.wait_ge(hi_ready, b * NS + n_split + 1)
                            nc.vector.scalar_tensor_tensor(rest[:, m, c0:c0 + cn], ps[:, bank, 0:cn], bias_s[:, m:m + 1],
                                                           parts[:, 0, m, c0:c0 + cn], ALU.add, ALU.subtract).then_inc(rest_ready, 1)
                            v.wait_ge(rest_ready, b * NS + n_split + 1)
                            v.sem_inc(dve_freed, 1)
                            n_split += 1
                            if n_split % 2 == 0 and converted < QT:
                                v.wait_ge(m_in[converted % 2], (b * (QT // 2) + converted // 2 + 1) * 16)
                                nc.vector.tensor_scalar(bias[:, converted, :], m_s[:, converted % 2, :], 0, MASKED,
                                                        ALU.is_equal, ALU.mult).then_inc(bias_ready, 1)
                                converted += 1
                        elif kind == "v":
                            v.wait_ge(filled, b * NJ + n + 1)
                            v.wait_ge(v_out, b * NG * 16)
                            tiles = 2 if i < KT - 1 else 1
                            r = P if i < KT - 1 else KLAST
                            for t in range(tiles):
                                last = nc.vector.tensor_tensor(
                                    vals[0:r, i + t, :, 0:DH],
                                    ps[0:r, bank, t * D:(t + 1) * D].rearrange("p (h c) -> p h c", h=H),
                                    bv_s[0:r, :].rearrange("p (h c) -> p h c", h=H), ALU.add)
                                if t == tiles - 1:
                                    last.then_inc(dve_freed, 1)
                    step = b * ROW_STEPS
                    v.wait_ge(act_freed, b * NA + jobs_act.index(("sum", 0, len(KEY_BLOCKS) - 1)) + 1)
                    v.wait_ge(row_out, b * 16)
                    nc.vector.scalar_tensor_tensor(maskodd[:, :], masksum[:, :], -float(S), masksum[:, :],
                                                   ALU.add, ALU.mult).then_inc(row_step, 1)
                    v.wait_ge(row_step, step + 1)
                    nc.vector.tensor_reduce(same[:, 0:1], maskodd[:, :], AX_X, ALU.min).then_inc(row_step, 1)
                    v.wait_ge(row_step, step + 2)
                    nc.vector.tensor_scalar(w["mixed"][:, bass.ds(b, 1)], same[:, 0:1], 0.0, None, ALU.is_lt).then_inc(row_step, 1)
                    nc.vector.tensor_scalar(same[:, 1:2], same[:, 0:1], 0.0, MASKED, ALU.is_ge, ALU.mult).then_inc(row_step, 1)
                    v.wait_ge(row_step, step + 4)
                    nc.vector.tensor_scalar(maskrow[:, :], masksum[:, :], float(S), None, ALU.is_equal).then_inc(row_step, 1)
                    v.wait_ge(row_step, step + 5)
                    nc.vector.tensor_scalar(maskrow[:, :], maskrow[:, :], same[:, 1:2], None, ALU.mult).then_inc(row_step, 1)

                batch(0)
                with nc.vector.Fori(1, B) as b:
                    batch(b)

            @block.tensor
            def _(pe):
                pe.wait_ge(consts_ready, 6)
                pe.wait_ge(ffn_scaled, FC + DC)
                for n in range(2 * DC):
                    for q in range(4):
                        c = (n % 2) * 4 + q
                        last = nc.tensor.transpose(ps[:, n, q * P:(q + 1) * P], w1_s[:, c, (n // 2) * P:(n // 2 + 1) * P], w["ident"][:, :])
                    last.then_inc(ffn_tr, 1)
                for n in range(2 * DC):
                    for q in range(4):
                        f, c = 2 * n + q // 2, q % 2
                        last = nc.tensor.transpose(ps[:, 2 * DC + n, q * P:(q + 1) * P], w2_s[:, c, f * P:(f + 1) * P], w["ident"][:, :])
                    last.then_inc(ffn_tr, 1)
                pe.wait_ge(ffn_kept, 4 * DC)
                pe.wait_ge(weights_in, 6 * 16)
                def batch(b):
                    for n, (kind, i, kb) in enumerate(jobs):
                        bank = n % 8
                        before, earlier = bank_before(n)
                        if not (earlier and first(b)):
                            if before in jobs_act:
                                pe.wait_ge(act_freed, b * NA + (jobs_act.index(before) + 1 - NA * earlier))
                            else:
                                pe.wait_ge(dve_freed, b * NV + (jobs_dve.index(before) + 1 - NV * earlier))
                        if kind == "cT":
                            if n == 0:
                                pe.wait_ge(c_in, 32 * b + 32)
                            if n == 0 and not first(b):
                                pe.wait_ge(dve_freed, b * NV)
                            k0, kn = KEY_BLOCKS[kb]
                            for q in range(0, kn, P):
                                r = min(P, kn - q)
                                last = nc.tensor.transpose(ps[:, bank, q:q + r], c_s[0:r, (k0 + q) // P, i * P:(i + 1) * P],
                                                           w["ident"][0:r, 0:r])
                        elif kind == "xT":
                            pe.wait_ge(xn_ready, b * QT + QT)
                            for q in range(QT):
                                last = nc.tensor.transpose(ps[:, bank, q * P:(q + 1) * P], xn[:, q, i * P:(i + 1) * P], w["ident"][:, :])
                        elif kind == "q":
                            pe.wait_ge(act_freed, b * NA + jobs_act.index(("xT", DC - 1, 0)) + 1)
                            for c in range(DC):
                                last = nc.tensor.matmul(ps[:, bank, :], wq_s[:, c, i * P:(i + 1) * P], xT[:, c, :],
                                                        start=c == 0, stop=c == DC - 1)
                        elif kind == "k":
                            k0, kn = KEY_BLOCKS[kb]
                            for c in range(DC):
                                last = nc.tensor.matmul(ps[:, bank, 0:kn], wk_s[:, c, i * P:(i + 1) * P], cT[:, c, k0:k0 + kn],
                                                        start=c == 0, stop=c == DC - 1)
                        elif kind == "v":
                            for t in range(2 if i < KT - 1 else 1):
                                r = keys_in(i + t)
                                for c in range(DC):
                                    last = nc.tensor.matmul(ps[0:r, bank, t * D:(t + 1) * D], cT[:, c, (i + t) * P:(i + t) * P + r],
                                                            wv_s[:, c, :], start=c == 0, stop=c == DC - 1)
                        elif kind == "sum":
                            k0, kn = KEY_BLOCKS[kb]
                            for q in range(QT):
                                last = nc.tensor.matmul(ps[0:1, bank, 0:kn], ones16[:, 0:1], bias[:, q, k0:k0 + kn],
                                                        start=q == 0, stop=q == QT - 1)
                        else:
                            pe.wait_ge(bias_ready, b * QT + QT)
                            for t in range(2 if i < KT - 1 else 1):
                                r = keys_in(i + t)
                                for q in range(QT):
                                    last = nc.tensor.transpose(psb[0:r, bank, t * S + q * P:t * S + (q + 1) * P],
                                                               bias[:, q, (i + t) * P:(i + t) * P + r], w["ident16"][:, :])
                        last.then_inc(filled, 1)

                batch(0)
                with nc.tensor.Fori(1, B) as b:
                    batch(b)


MC = QT * HG * NCH
EARLY = 10
LATE = 4


def order(next1, next2):
    chunks = [("C1", m) for m in range(EARLY, MC)] * next1 + [("C2", m) for m in range(EARLY)] * next2
    slots = 3 * KT
    due = {}
    for k, c in enumerate(chunks):
        due.setdefault(k * slots // MC, []).append(c)
    t_slot = (MC - EARLY - 1) * slots // MC + LATE
    steps, slot = [], 0

    def fill():
        nonlocal slot
        steps.extend(due.get(slot, []))
        if next1 and slot == t_slot:
            steps.append(("T", 0))
        slot += 1

    for kt in range(KT):
        steps.extend([("S", kt, 0), ("S", kt, 1)])
        fill()
        steps.extend([("S", kt, 2), ("S", kt, 3)])
        fill()
        steps.append(("V", kt - 1))
        fill()
    return steps


def units(steps):
    return [x for x in steps if x[0] in "ST"]


RING = 3
UNITS = KT * HG + 1
BATCH_UNITS = NG * UNITS


def attend(nc, w, g_attn, g_ffn, wo, bo, b1, b2, kparts_d, qparts_d, values_d, bias_d, biasT_d, maskrow_d, ones_d, zeros_d,
           heads_d, sums_d, recips_d):
    with ExitStack() as es:
        def sb(name, shape, dt=F32):
            return es.enter_context(nc.sbuf_tensor(name, shape, dt))

        def sem(name):
            return es.enter_context(nc.semaphore(name))

        kst = [sb(f"kst{g}", [P, HG, SK], BF16) for g in range(NG)]
        qst = [sb(f"qst{g}", [P, HG, S], BF16) for g in range(NG)]
        vst = [sb(f"vst{g}", [P, KT, HG * 2 * DH]) for g in range(NG)]
        bias, biasT = sb("bias2", [P, QT, SK], BF16), sb("biasT2", [P, KT, S], BF16)
        PR = 3
        probs = sb("probs", [P, PR, HG, S])
        outs = sb("outs", [P, 2, S])
        junk = sb("junk", [P, 2, CW], BF16)
        cmax = sb("cmax", [P, 2, QT * HG, NCH])
        negmax, rest = sb("negmax", [P, 2, QT * HG]), sb("rest", [P, 2, QT * HG])
        mparts, mrows = sb("mparts", [P, P // (QT * HG), QT * HG], BF16), sb("mrows", [PARTS * QT * HG, P], BF16)
        wo_s, bo_s, gate, b1_s, b2_s = w["wo"], w["bo"], w["gate"], w["b1"], w["b2"]
        sums, recips = sb("sums2", [P, (B - 1) * H * S // P]), sb("recips2", [P, (B - 1) * H * S // P])
        ps_s = es.enter_context(nc.psum_tensor("ps_s", [P, RING, S], F32))
        ps_m = es.enter_context(nc.psum_tensor("ps_m", [P, 2, 2 * 512], F32))
        ps_o = es.enter_context(nc.psum_tensor("ps_o", [P, S], F32))
        ps_tr = ps_s[:, :, :].bitcast(BF16)

        mparts_init, wait_carrier = sem("mparts_init"), sem("wait_carrier")
        rows_in, mask_rows_in = sem("rows_in"), sem("mask_rows_in")
        wo_zeroed, consts_in, gates_ready, biases_gated = sem("wo_zeroed"), sem("consts_in"), sem("gates_ready"), sem("biases_gated")
        stack_in = [sem(f"stack_in{g}") for g in range(NG)]
        bias_in = [sem(f"bias_in{t}") for t in range(QT)]
        biasT_in = sem("biasT_in")
        scored, freed, summed, out_kept = sem("scored"), sem("freed"), sem("summed"), sem("out_kept")
        out_stored = [sem("out_stored0"), sem("out_stored1")]
        max_scored, max_taken = sem("max_scored"), sem("max_taken")
        max_step, max_parts, max_in = sem("max_step"), sem("max_parts"), sem("max_in")
        sums_in, recips_step, recips_out = sem("sums_in"), sem("recips_step"), sem("recips_out")
        NDMA = 2 * len(STACK) - 2 + 2
        STEPS = 6

        def group_steps(last, g):
            return order(not (last and g == NG - 1), not (last and g >= NG - 2))

        def unit_base(b):
            return b * BATCH_UNITS + 1

        def transposed_unit(b, g, last):
            return unit_base(b) + g * UNITS + units(group_steps(last, g)).index(("T", 0)) + 1

        def batch_of(b, g):
            return b if g < NG else b + 1

        def load_stack(sp, g, gi, b):
            def rows(t, r0, r1):
                return t[r0:r1, :, :].rearrange("p h c -> p (h c)")

            kd, qd = kparts_d[gi, :, :, :, :].rearrange("a d h c -> (a d) (h c)"), qparts_d[gi, :, :, :, :].rearrange("a d h c -> (a d) (h c)")
            for dst, r0, r1, src, s0 in ((kst[g], 0, 16, kd, 0), (kst[g], 32, 64, kd, DH), (kst[g], 64, 96, kd, 0), (kst[g], 96, 112, kd, 0),
                                         (qst[g], 0, 16, qd, 0), (qst[g], 32, 48, qd, 0), (qst[g], 48, 64, qd, 0),
                                         (qst[g], 64, 80, qd, DH), (qst[g], 80, 96, qd, DH), (qst[g], 96, 112, qd, 2 * DH)):
                sp.dma_start(rows(dst, r0, r1), src[s0:s0 + r1 - r0, :]).then_inc(stack_in[g], 16)
            mrow = maskrow_d[bass.ds(b, 1), :].rearrange("a (h c) -> a h c", h=1).to_broadcast([1, HG, SK])
            sp.dma_start(kst[g][MASK_ROW:MASK_ROW + 1, :, :], mrow).then_inc(stack_in[g], 16)
            sp.dma_start(vst[g][:, :, :], values_d[gi, :, :, :]).then_inc(stack_in[g], 16)

        def max_rows_in(sp, g, copied):
            sp.wait_ge(freed, copied)
            for p in range(PARTS):
                sp.dma_start(qst[g][MAX_ROW + p:MAX_ROW + p + 1, :, :].rearrange("p h c -> p (h c)"),
                             mrows[p * QT * HG:(p + 1) * QT * HG, :]).then_inc(max_in, 16)

        with nc.Block() as block:
            @block.sync
            def _(sp):
                for g in range(NG):
                    for r0, filled_in in ((MAX_ROW, rows_in), (MASK_ROW, mask_rows_in)):
                        sp.dma_start(kst[g][r0:r0 + DH, :, :], ones_d[:, :, :]).then_inc(filled_in, 16)
                    sp.dma_start(qst[g][MASK_ROW:MASK_ROW + DH, :, :], zeros_d[:, :, :]).then_inc(mask_rows_in, 16)
                    sp.dma_start(qst[g][MAX_ROW + PARTS:P, :, :], zeros_d[1:1 + P - MAX_ROW - PARTS, :, :]).then_inc(rows_in, 16)
                    sp.wait_ge(mask_rows_in, (g + 1) * 32)
                    load_stack(sp, g, g, 0)
                sp.wait_ge(wo_zeroed, 1)
                for g in range(NG):
                    for h in range(HG):
                        r0 = (g * HG + h) * DH
                        sp.dma_start(wo_s[2 * DH * h:2 * DH * h + DH, g, :], wo[r0:r0 + DH, :]).then_inc(consts_in, 16)
                for dst, src in ((bo_s, bo), (b2_s, b2)):
                    sp.dma_start(dst[:, :], src.rearrange("(a d) -> a d", a=1).to_broadcast([P, D])).then_inc(consts_in, 16)
                sp.dma_start(b1_s[:, :], b1.rearrange("(c p) -> p c", p=P), allow_slow_non_contiguous=True).then_inc(consts_in, 16)
                for k, src in enumerate((g_attn, g_ffn)):
                    sp.dma_start(gate[:, k:k + 1], src.rearrange("(a d) -> a d", a=1).to_broadcast([P, 1])).then_inc(consts_in, 16)
                max_rows_in(sp, 0, 1)

                def batch(b, last):
                    for g in range(NG):
                        if not (last and g == NG - 1):
                            max_rows_in(sp, (g + 1) % NG, transposed_unit(b, g, last))
                        if not last:
                            sp.wait_ge(summed, (b * NG + g + 1) * KT)
                            load_stack(sp, g, b * NG + g + NG, b + 1)
                        if last and g == 1:
                            for stored in out_stored:
                                sp.wait_ge(stored, (B - 1) * NG // 2 * 32)
                            sp.dma_start(sums[:, :], sums_d[0:B - 1, :, :].rearrange("b h s -> (b h s)").rearrange("(p c) -> p c", p=P)).then_inc(sums_in, 16)
                            sp.wait_ge(recips_step, 1)
                            sp.dma_start(recips_d[0:B - 1, :, :].rearrange("b h s -> (b h s)").rearrange("(p c) -> p c", p=P), recips[:, :]).then_inc(recips_out, 16)

                batch(0, False)
                with nc.sync.Fori(1, B - 1) as b:
                    batch(b, False)
                batch(B - 1, True)
                sp.wait_ge(recips_out, 16)

            @block.gpsimd
            def _(pool):
                for qt in range(QT):
                    pool.dma_start(bias[:, qt, :], bias_d[0, :, qt, :]).then_inc(bias_in[qt], 16)
                pool.dma_start(biasT[:, :, :], biasT_d[0, :, :, :]).then_inc(biasT_in, 16)
                nc.gpsimd.memset(wo_s[:, :, :], 0.0).then_inc(wo_zeroed, 1)
                pool.wait_ge(gates_ready, 1)
                nc.gpsimd.tensor_scalar(bo_s[:, :], bo_s[:, :], gate[:, 0:1], None, ALU.mult).then_inc(biases_gated, 1)
                nc.gpsimd.tensor_scalar(b2_s[:, :], b2_s[:, :], gate[:, 1:2], None, ALU.mult).then_inc(biases_gated, 1)

                def store(b, g):
                    pool.wait_ge(out_kept, b * NG + g + 1)
                    pool.dma_start(heads_d[b * NG + g, :, :], outs[:, g % 2, :]).then_inc(out_stored[g % 2], 16)
                    pool.dma_start(sums_d[b, g * HG:(g + 1) * HG, :], outs[DH::2 * DH, g % 2, :]).then_inc(out_stored[g % 2], 16)

                def next_bias(b, qt):
                    pool.wait_ge(max_taken, (b * NG + NG - 1) * MC + (qt + 1) * HG * NCH)
                    pool.dma_start(bias[:, qt, :], bias_d[b + 1, :, qt, :]).then_inc(bias_in[qt], 16)

                def batch(b, last):
                    store(b, 0)
                    if not last:
                        next_bias(b, 0)
                    store(b, 1)
                    if not last:
                        for qt in range(1, QT):
                            next_bias(b, qt)
                    store(b, 2)
                    store(b, 3)
                    if not last:
                        pool.wait_ge(scored, unit_base(b + 1))
                        pool.dma_start(biasT[:, :, :], biasT_d[b + 1, :, :, :]).then_inc(biasT_in, 16)

                batch(0, False)
                with nc.gpsimd.Fori(1, B - 1) as b:
                    batch(b, False)
                batch(B - 1, True)
                for stored in out_stored:
                    pool.wait_ge(stored, B * NG // 2 * 32)

            @block.scalar
            def _(act):
                def copy_maxima(b_unit, n):
                    act.wait_ge(scored, b_unit + n + 1)
                    nc.scalar.activation(mrows[:, :], ps_tr[0:PARTS * QT * HG, n % RING, 0:P], ACT.Copy).then_inc(freed, 1)

                copy_maxima(0, 0)
                act.wait_ge(consts_in, (NG * HG + 5) * 16)
                nc.scalar.activation(gate[:, :], gate[:, :], ACT.Tanh).then_inc(gates_ready, 1)

                def batch(b, last):
                    n = 0
                    for g in range(NG):
                        for step in units(group_steps(last, g)):
                            if step[0] == "T":
                                act.wait_ge(max_in, (b * NG + g + 1) * PARTS * 16)
                                copy_maxima(unit_base(b), n)
                            else:
                                kt, h = step[1:]
                                tile, r = g * KT + kt, keys_in(kt)
                                act.wait_ge(scored, unit_base(b) + n + 1)
                                if h == 0:
                                    act.wait_ge(summed, b * NG * KT + max(tile - PR + 1, 0))
                                nc.scalar.activation(probs[0:r, tile % PR, h, :], ps_s[0:r, n % RING, :],
                                                     ACT.Exp, scale=SCALE).then_inc(freed, 1)
                            n += 1

                batch(0, False)
                with nc.scalar.Fori(1, B - 1) as b:
                    batch(b, False)
                batch(B - 1, True)

            @block.vector
            def _(v):
                def take_max(g, gi, bi, m):
                    qt, h, c = m // (HG * NCH), (m // NCH) % HG, m % NCH
                    c0, cn = CHUNKS[c]
                    if m % (HG * NCH) == 0:
                        v.wait_ge(bias_in[qt], bi * 16 + 16)
                    v.wait_ge(max_scored, gi * MC + m + 1)
                    v.sem_inc(wait_carrier, 1)
                    nc.vector.tensor_tensor_reduce(junk[:, m % 2, 0:cn], ps_m[:, m % 2, 0:cn], bias[:, qt, c0:c0 + cn], 1.0, LOWEST,
                                                   ALU.add, ALU.max, cmax[:, g % 2, h * QT + qt, c:c + 1]).then_inc(max_taken, 1)

                def split_max(g, gi):
                    base = gi * STEPS
                    v.wait_ge(max_taken, (gi + 1) * MC)
                    nc.vector.tensor_reduce(negmax[:, 0, :], cmax[:, g % 2, :, :], AX_X, ALU.max).then_inc(max_step, 1)
                    v.wait_ge(max_step, base + 1)
                    nc.vector.tensor_scalar(negmax[:, 1, :], negmax[:, 0, :], MASKED, -1.0, ALU.max, ALU.mult).then_inc(max_step, 1)
                    v.wait_ge(max_in, gi * PARTS * 16)
                    v.wait_ge(max_step, base + 2)
                    nc.vector.tensor_copy(mparts[:, 0, :], negmax[:, 1, :]).then_inc(max_step, 1)
                    v.wait_ge(max_step, base + 3)
                    nc.vector.tensor_tensor(rest[:, 0, :], negmax[:, 1, :], mparts[:, 0, :], ALU.subtract).then_inc(max_step, 1)
                    v.wait_ge(max_step, base + 4)
                    nc.vector.tensor_copy(mparts[:, 1, :], rest[:, 0, :]).then_inc(max_step, 1)
                    v.wait_ge(max_step, base + 5)
                    nc.vector.tensor_tensor(rest[:, 1, :], rest[:, 0, :], mparts[:, 1, :], ALU.subtract).then_inc(max_step, 1)
                    v.wait_ge(max_step, base + 6)
                    nc.vector.tensor_copy(mparts[:, 2, :], rest[:, 1, :]).then_inc(max_parts, 1)

                def keep_output(b, g):
                    v.wait_ge(summed, (b * NG + g + 1) * KT)
                    v.wait_ge(out_stored[g % 2], (b * (NG // 2) + g // 2) * 32)
                    nc.vector.tensor_copy(outs[:, g % 2, :], ps_o[:, :]).then_inc(out_kept, 1)

                nc.vector.memset(mparts[:, :, :], 0.0).then_inc(mparts_init, 1)
                v.wait_ge(mparts_init, 1)
                for m in range(MC):
                    take_max(0, 0, 0, m)
                split_max(0, 0)
                for m in range(EARLY):
                    take_max(1, 1, 0, m)

                def batch(b, last):
                    for g in range(NG):
                        gi = b * NG + g
                        next1, next2 = not (last and g == NG - 1), not (last and g >= NG - 2)
                        for m in range(EARLY, MC) if next1 else ():
                            take_max((g + 1) % NG, gi + 1, batch_of(b, g + 1), m)
                            if g > 0 and m == EARLY + 2:
                                keep_output(b, g - 1)
                        if not next1:
                            keep_output(b, g - 1)
                        if next1:
                            split_max((g + 1) % NG, gi + 1)
                        for m in range(EARLY) if next2 else ():
                            take_max((g + 2) % NG, gi + 2, batch_of(b, g + 2), m)
                        if last and g == 1:
                            v.wait_ge(sums_in, 16)
                            nc.vector.reciprocal(recips[:, :], sums[:, :]).then_inc(recips_step, 1)
                    keep_output(b, NG - 1)

                batch(0, False)
                with nc.vector.Fori(1, B - 1) as b:
                    batch(b, False)
                batch(B - 1, True)

            @block.tensor
            def _(pe):
                def score_for_max(g, gi, bi, m):
                    if m == 0:
                        pe.wait_ge(stack_in[g], bi * NDMA * 16 + NDMA * 16)
                    if not (type(gi) is int and gi * MC + m < 2):
                        pe.wait_ge(max_taken, gi * MC + m - 1)
                    qt, h, c = m // (HG * NCH), (m // NCH) % HG, m % NCH
                    c0, cn = CHUNKS[c]
                    for a in range(0, cn, 512):
                        an = min(512, cn - a)
                        last = nc.tensor.matmul(ps_m[:, m % 2, a:a + an], qst[g][0:MAX_ROW, h, qt * P:(qt + 1) * P],
                                                kst[g][0:MAX_ROW, h, c0 + a:c0 + a + an], start=True, stop=True)
                    last.then_inc(max_scored, 1)

                def take_bank(b_unit, n):
                    pe.wait_ge(freed, b_unit + max(n - RING + 1, 0))

                def transpose_max(gi, n):
                    pe.wait_ge(max_parts, gi + 1)
                    nc.tensor.transpose(ps_tr[:, n % RING, 0:P], mparts[:, :, :].rearrange("p a n -> p (a n)"),
                                        w["ident16"][:, :]).then_inc(scored, 1)

                def score(g, kt, h, n, mixed):
                    r = keys_in(kt)
                    last = nc.tensor.matmul(ps_s[0:r, n % RING, :], kst[g][:, h, kt * P:kt * P + r], qst[g][:, h, :],
                                            start=True, stop=not mixed)
                    if mixed:
                        last = nc.tensor.matmul(ps_s[0:r, n % RING, :], w["ident16"][0:r, 0:r], biasT[0:r, kt, :],
                                                start=False, stop=True)
                    last.then_inc(scored, 1)

                def sum_tile(b, g, kt, tile, exps):
                    r = keys_in(kt)
                    pe.wait_ge(freed, exps)
                    if kt == 0:
                        pe.wait_ge(out_kept, b * NG + g)
                    for h in range(HG):
                        strip = slice(2 * DH * h, 2 * DH * (h + 1))
                        last = nc.tensor.matmul(ps_o[strip, :], vst[g][0:r, kt, strip], probs[0:r, tile % PR, h, :],
                                                start=kt == 0, stop=kt == KT - 1)
                    last.then_inc(summed, 1)

                for m in range(MC):
                    score_for_max(0, 0, 0, m)
                transpose_max(0, 0)
                for m in range(EARLY):
                    score_for_max(1, 1, 0, m)

                def batch(b, last, mixed):
                    n, tail = 0, {}
                    if mixed:
                        pe.wait_ge(biasT_in, b * 16 + 16)
                    for g in range(NG):
                        gi = b * NG + g
                        pe.wait_ge(max_in, (gi + 1) * PARTS * 16)
                        for step in group_steps(last, g):
                            if step[0] == "S":
                                take_bank(unit_base(b), n)
                                score(g, step[1], step[2], n, mixed)
                                n += 1
                                tail[g * KT + step[1]] = unit_base(b) + n
                            elif step[0] == "T":
                                take_bank(unit_base(b), n)
                                transpose_max(gi + 1, n)
                                n += 1
                            elif step[0] == "V":
                                tile = g * KT + step[1]
                                if tile >= 0:
                                    sum_tile(b, tile // KT, tile % KT, tile, tail[tile])
                            else:
                                ahead = int(step[0][1])
                                score_for_max((g + ahead) % NG, gi + ahead, batch_of(b, g + ahead), step[1])
                    sum_tile(b, NG - 1, KT - 1, NG * KT - 1, tail[NG * KT - 1])

                pe.wait_ge(rows_in, NG * 32)

                def either(b, last):
                    mixed = nc.tensor.value_load(w["mixed"][0:1, bass.ds(b, 1)], min_val=0, max_val=1)
                    with nc.tensor.If(mixed != 0):
                        batch(b, last, True)
                    with nc.tensor.Else():
                        batch(b, last, False)

                either(0, False)
                with nc.tensor.Fori(1, B - 1) as b:
                    either(b, False)
                either(B - 1, True)


def finish(nc, w, x, heads_d, sums_d, recips_d, out):
    with ExitStack() as es:
        def sb(name, shape, dt=F32):
            return es.enter_context(nc.sbuf_tensor(name, shape, dt))

        def sem(name):
            return es.enter_context(nc.semaphore(name))

        wo_s, bo_s, gate, b1_s, b2_s = w["wo"], w["bo"], w["gate"], w["b1"], w["b2"]
        sums, recips = sb("sums3", [P, H * S // P]), sb("recips3", [P, H * S // P])
        heads, recip = sb("heads", [P, 2, NG, S]), sb("recip", [P, 2, NG, S])
        x_s, xb = sb("x3", [P, 2, QT, D]), sb("xb3", [P, B, QT, D])
        x1, xn = sb("x1", [P, B, QT, D]), sb("xn3", [P, B, QT, D])
        stats, mean_var, rstd = sb("stats3", [P, QT, 6]), sb("mean_var3", [P, QT, 2]), sb("rstd3", [P, QT, 2])
        xT, hT = sb("xT3", [P, 2, DC, S]), sb("hT3", [P, 2, FC, S])
        y = sb("y3", [P, 2, QT, D])
        ps_y = es.enter_context(nc.psum_tensor("ps_y", [P, 2, S], F32))
        ps_t = es.enter_context(nc.psum_tensor("ps_xt", [P, 2, S], F32))
        ps_h = es.enter_context(nc.psum_tensor("ps_h", [P, 4, S], F32))

        init = sem("init3")
        sums_in, recips_ready, recips_out = sem("sums_in3"), sem("recips_ready"), sem("recips_out3")
        heads_in, x_in = [sem("heads_in0"), sem("heads_in1")], [sem("x_in0"), sem("x_in1")]
        scaled, projected, xb_ready, x1_ready = sem("scaled"), sem("projected"), sem("xb_ready"), sem("x1_ready")
        ln_step, var_ready, std_ready, xn_ready = sem("ln_step3"), sem("var_ready3"), sem("std_ready3"), sem("xn_ready3")
        xb2_ready, transposed, xT_ready, hidden, gelu_ready, added, y_ready = (
            sem("xb2_ready"), sem("transposed"), sem("xT_ready"), sem("hidden"), sem("gelu_ready"), sem("added"), sem("y_ready"))
        y_out = [sem("y_out0"), sem("y_out1")]

        with nc.Block() as block:
            @block.sync
            def _(sp):
                def load_batch(b):
                    if b >= 2:
                        sp.wait_ge(projected, (b - 1) * QT)
                        sp.wait_ge(xb_ready, b - 1)
                    sp.dma_start(heads[:, b % 2, :, :], heads_d[b * NG:(b + 1) * NG, :, :].rearrange("g p c -> p g c")).then_inc(heads_in[b % 2], 16)
                    for h in range(HG):
                        src = recips_d[b, :, :].rearrange("(a g h) s -> a h g s", a=1, h=HG)[:, h, :, :].to_broadcast([DH, NG, S])
                        sp.dma_start(recip[2 * DH * h:2 * DH * h + DH, b % 2, :, :], src).then_inc(heads_in[b % 2], 16)
                    sp.dma_start(x_s[:, b % 2, :, :], x[b, :, :].rearrange("(t p) d -> p t d", p=P)).then_inc(x_in[b % 2], 16)

                sp.dma_start(sums[:, :], sums_d[B - 1, :, :].rearrange("h s -> (h s)").rearrange("(p c) -> p c", p=P)).then_inc(sums_in, 16)
                sp.wait_ge(init, 1)
                load_batch(0)
                load_batch(1)
                sp.wait_ge(recips_ready, 1)
                sp.dma_start(recips_d[B - 1, :, :].rearrange("h s -> (h s)").rearrange("(p c) -> p c", p=P), recips[:, :]).then_inc(recips_out, 16)
                load_batch(2)
                sp.wait_ge(recips_out, 16)
                load_batch(3)

            @block.gpsimd
            def _(pool):
                nc.gpsimd.memset(recip[:, :, :, :], 0.0).then_inc(init, 1)

                def scale_heads(b):
                    pool.wait_ge(heads_in[b % 2], (HG + 1) * 16 * (b // 2) + (HG + 1) * 16)
                    for g in range(NG):
                        nc.gpsimd.tensor_tensor(heads[:, b % 2, g, :], heads[:, b % 2, g, :], recip[:, b % 2, g, :], ALU.mult).then_inc(scaled, 1)

                def add_biases(b):
                    pool.wait_ge(x_in[b % 2], 16 * (b // 2) + 16)
                    for t in range(QT):
                        last = nc.gpsimd.tensor_tensor(xb[:, b, t, :], x_s[:, b % 2, t, :], bo_s[:, :], ALU.add)
                    last.then_inc(xb_ready, 1)

                scale_heads(0)
                add_biases(0)
                for b in range(1, B):
                    scale_heads(b)
                    add_biases(b)
                for b in range(B):
                    pool.wait_ge(x1_ready, (b + 1) * QT)
                    for t in range(QT):
                        last = nc.gpsimd.tensor_tensor(xb[:, b, t, :], x1[:, b, t, :], b2_s[:, :], ALU.add)
                    last.then_inc(xb2_ready, 1)
                for b in range(B):
                    pool.wait_ge(y_ready, (b + 1) * QT)
                    pool.dma_start(out[b, :, :].rearrange("(t p) d -> p t d", p=P), y[:, b % 2, :, :]).then_inc(y_out[b % 2], 16)
                for stored in y_out:
                    pool.wait_ge(stored, B // 2 * 16)

            @block.scalar
            def _(act):
                for b in range(B):
                    act.wait_ge(var_ready, b + 1)
                    nc.scalar.activation(rstd[:, :, 0], rstd[:, :, 0], ACT.Sqrt).then_inc(std_ready, 1)
                for b in range(B):
                    if b >= 2:
                        act.wait_ge(added, (b - 1) * QT)
                    for f in range(FC):
                        act.wait_ge(hidden, b * FC + f + 1)
                        nc.scalar.activation(hT[:, b % 2, f, :], ps_h[:, f % 4, :], ACT.Gelu, bias=b1_s[:, f:f + 1]).then_inc(gelu_ready, 1)

            @block.vector
            def _(v):
                v.wait_ge(sums_in, 16)
                nc.vector.reciprocal(recips[:, :], sums[:, :]).then_inc(recips_ready, 1)
                for b in range(B):
                    v.wait_ge(xb_ready, b + 1)
                    for t in range(QT):
                        v.wait_ge(projected, b * QT + t + 1)
                        nc.vector.scalar_tensor_tensor(x1[:, b, t, :], ps_y[:, t % 2, 0:D], gate[:, 0:1], xb[:, b, t, :],
                                                       ALU.mult, ALU.add).then_inc(x1_ready, 1)
                    base = b * (2 * QT + 1)
                    for t in range(QT):
                        v.wait_ge(x1_ready, b * QT + t + 1)
                        nc.vector.bn_stats(stats[:, t, :], x1[:, b, t, :]).then_inc(ln_step, 1)
                    v.wait_ge(ln_step, base + QT)
                    for t in range(QT):
                        nc.vector.bn_aggr(mean_var[:, t, :], stats[:, t, :]).then_inc(ln_step, 1)
                    v.wait_ge(ln_step, base + 2 * QT)
                    layernorm_scales(nc, v, mean_var, rstd, var_ready, std_ready, ln_step, base + 2 * QT + 1, b)
                    for t in range(QT):
                        nc.vector.tensor_scalar(xn[:, b, t, :], x1[:, b, t, :], mean_var[:, t, 0:1], rstd[:, t, 1:2],
                                                ALU.subtract, ALU.mult).then_inc(xn_ready, 1)

                def keep_xT(b):
                    if b >= 2:
                        v.wait_ge(hidden, (b - 1) * FC)
                    for c in range(DC):
                        v.wait_ge(transposed, b * DC + c + 1)
                        nc.vector.tensor_copy(xT[:, b % 2, c, :], ps_t[:, c, :]).then_inc(xT_ready, 1)

                keep_xT(0)
                for b in range(B):
                    if b + 1 < B:
                        keep_xT(b + 1)
                    v.wait_ge(xb2_ready, b + 1)
                    if b >= 2:
                        v.wait_ge(y_out[b % 2], b // 2 * 16)
                    for t in range(QT):
                        v.wait_ge(added, b * QT + t + 1)
                        nc.vector.scalar_tensor_tensor(y[:, b % 2, t, :], ps_y[:, t % 2, 0:D], gate[:, 1:2], xb[:, b, t, :],
                                                       ALU.mult, ALU.add).then_inc(y_ready, 1)

            @block.tensor
            def _(pe):
                for b in range(B):
                    pe.wait_ge(scaled, (b + 1) * NG)
                    for t in range(QT):
                        if b * QT + t >= 2:
                            pe.wait_ge(x1_ready, b * QT + t - 1)
                        for g in range(NG):
                            last = nc.tensor.matmul(ps_y[:, t % 2, 0:D], heads[:, b % 2, g, t * P:(t + 1) * P], wo_s[:, g, :],
                                                    start=g == 0, stop=g == NG - 1)
                        last.then_inc(projected, 1)

                def transposes(b):
                    pe.wait_ge(xn_ready, (b + 1) * QT)
                    if b:
                        pe.wait_ge(xT_ready, b * DC)
                    for c in range(DC):
                        for t in range(QT):
                            last = nc.tensor.transpose(ps_t[:, c, t * P:(t + 1) * P], xn[:, b, t, c * P:(c + 1) * P], w["ident"][:, :])
                        last.then_inc(transposed, 1)

                def widen(b):
                    pe.wait_ge(xT_ready, (b + 1) * DC)
                    for f in range(FC):
                        if b * FC + f >= 4:
                            pe.wait_ge(gelu_ready, b * FC + f - 3)
                        for c in range(DC):
                            last = nc.tensor.matmul(ps_h[:, f % 4, :], w["w1T"][:, c, f * P:(f + 1) * P], xT[:, b % 2, c, :],
                                                    start=c == 0, stop=c == DC - 1)
                        last.then_inc(hidden, 1)

                def narrow(b):
                    pe.wait_ge(gelu_ready, (b + 1) * FC)
                    for t in range(QT):
                        if b == 0 and t < 2:
                            pe.wait_ge(x1_ready, B * QT)
                        else:
                            pe.wait_ge(y_ready, b * QT + t - 1)
                        for f in range(FC):
                            last = nc.tensor.matmul(ps_y[:, t % 2, 0:D], hT[:, b % 2, f, t * P:(t + 1) * P], w["w2T"][:, f, :],
                                                    start=f == 0, stop=f == FC - 1)
                        last.then_inc(added, 1)

                transposes(0)
                for b in range(B):
                    if b + 1 < B:
                        transposes(b + 1)
                    widen(b)
                    if b:
                        narrow(b - 1)
                narrow(B - 1)


def gated_cross_attention_block(nc, x, ctx_in, mask, g_attn, g_ffn, wq, bq, wk, bk, wv, bv, wo, bo, w1, b1, w2, b2, out):
    def dram(name, shape, dt=F32):
        return nc.dram_tensor(name, shape, dt, kind="Internal").ap()

    kparts_d = dram("kparts_d", (B * NG, PARTS, DH, HG, SK), BF16)
    qparts_d = dram("qparts_d", (B * NG, PARTS, DH, HG, S), BF16)
    values_d = dram("values_d", (B * NG, P, KT, HG * 2 * DH))
    bias_d = dram("bias_d", (B, P, QT, SK), BF16)
    biasT_d = dram("biasT_d", (B, P, KT, S), BF16)
    heads_d = dram("heads_d", (B * NG, P, S))
    sums_d, recips_d = dram("sums_d", (B, H, S)), dram("recips_d", (B, H, S))
    ones_d, zeros_d = dram("ones_d", (DH, HG, SK), BF16), dram("zeros_d", (DH, HG, S), BF16)
    maskrow_d = dram("maskrow_d", (B, SK), BF16)
    with ExitStack() as es:
        w = {
            "ident": es.enter_context(nc.sbuf_tensor("ident", [P, P], F32)),
            "ident16": es.enter_context(nc.sbuf_tensor("ident16", [P, P], BF16)),
            "wo": es.enter_context(nc.sbuf_tensor("wo_s", [P, NG, D], F32)),
            "bo": es.enter_context(nc.sbuf_tensor("bo_s", [P, D], F32)),
            "gate": es.enter_context(nc.sbuf_tensor("gate", [P, 2], F32)),
            "b1": es.enter_context(nc.sbuf_tensor("b1_s", [P, FC], F32)),
            "b2": es.enter_context(nc.sbuf_tensor("b2_s", [P, D], F32)),
            "mixed": es.enter_context(nc.sbuf_tensor("mixed", [1, B], I32)),
            "w1T": es.enter_context(nc.sbuf_tensor("w1T", [P, DC, F], F32)),
            "w2T": es.enter_context(nc.sbuf_tensor("w2T", [P, FC, D], F32)),
        }
        prepare(nc, w, x, ctx_in, mask, wq, bq, wk, bk, wv, bv, w1, w2, kparts_d, qparts_d, values_d, bias_d, biasT_d, maskrow_d,
                ones_d, zeros_d)
        attend(nc, w, g_attn, g_ffn, wo, bo, b1, b2, kparts_d, qparts_d, values_d, bias_d, biasT_d, maskrow_d, ones_d, zeros_d,
               heads_d, sums_d, recips_d)
        finish(nc, w, x, heads_d, sums_d, recips_d, out)


_INS = ["x", "ctx_1024", "mask_BxSxS2_ik1", "g_xattn", "g_ffn", "L0_xattn_Wq", "L0_xattn_bq", "L0_xattn_Wk", "L0_xattn_bk",
        "L0_xattn_Wv", "L0_xattn_bv", "L0_xattn_Wo", "L0_xattn_bo", "L0_ffn_w1", "L0_ffn_b1", "L0_ffn_w2", "L0_ffn_b2"]


def kernel(**inputs):
    import numpy as _np
    import concourse.bacc as _bacc
    from concourse import mybir as _mybir
    from concourse.bass_utils import run_bass_kernel_spmd as _run

    nc = _bacc.Bacc("TRN2", target_bir_lowering=False, num_devices=1)
    arrays, args = {}, []
    for name in _INS:
        a = _np.ascontiguousarray(inputs[name])
        arrays[f"in_{name}_dram"] = a
        args.append(nc.dram_tensor(f"in_{name}_dram", a.shape, _mybir.dt.from_np(a.dtype), kind="ExternalInput").ap())
    args.append(nc.dram_tensor("out_0_dram", (B, S, D), F32, kind="ExternalOutput").ap())
    gated_cross_attention_block(nc, *args)
    r = _run(nc, [arrays], core_ids=[0])
    return r.results[0]["out_0_dram"]
```

```python
from contextlib import ExitStack

import concourse.bass as bass
from concourse import mybir

ALU = mybir.AluOpType
ACT = mybir.ActivationFunctionType
AX_X = mybir.AxisListType.X
F32 = mybir.dt.float32
BF16 = mybir.dt.bfloat16
I32 = mybir.dt.int32

P = 128
B, S, D = 4, 512, 256
SK = 1601
H, DH = 16, 16
F = 1024
DC = D // P
QT = S // P
FC = F // P
KT = -(-SK // P)
KLAST = SK - (KT - 1) * P
HG = 4
NG = H // HG
GR = HG * DH
PARTS = 3
SCALE = float(DH) ** -0.5
MASKED = -(2.0 ** 100)
LOWEST = -3.0e38
LN_EPS = 1e-5

STACK = [(0, 0, 0), (32, 0, 1), (48, 0, 2), (64, 1, 0), (80, 1, 1), (96, 2, 0)]
MASK_ROW = 16
MAX_ROW = 112

KEY_BLOCKS = [(k, min(512, SK - k)) for k in range(0, SK, 512)]
NCH = 2
CW = -(-SK // NCH)
CHUNKS = [(c * CW, min(CW, SK - c * CW)) for c in range(NCH)]


def keys_in(kt):
    return KLAST if kt == KT - 1 else P


def layernorm_scales(nc, v, mean_var, rstd, var_ready, std_ready, step, base, index):
    nc.vector.tensor_scalar(rstd[:, :, 0], mean_var[:, :, 1], LN_EPS, None, ALU.add).then_inc(var_ready, 1)
    v.wait_ge(std_ready, index + 1)
    nc.vector.reciprocal(rstd[:, :, 1], rstd[:, :, 0]).then_inc(step, 1)
    v.wait_ge(step, base)


def prepare(nc, w, x, ctx_in, mask, wq, bq, wk, bk, wv, bv, w1, w2, alpha2_d, kparts_d, qparts_d, values_d, bias_d, biasT_d,
            maskrow_d, ones_d, zeros_d):
    with ExitStack() as es:
        def sb(name, shape, dt=F32):
            return es.enter_context(nc.sbuf_tensor(name, shape, dt))

        def sem(name):
            return es.enter_context(nc.semaphore(name))

        wq_s, wk_s, wv_s = sb("wq_s", [P, DC, D]), sb("wk_s", [P, DC, D]), sb("wv_s", [P, DC, D])
        bq_s, bk_s, bv_s = sb("bq_s", [P, DC]), sb("bk_s", [P, DC]), sb("bv_s", [P, D])
        x_s, xn, xT = sb("x_s", [P, QT, D]), sb("xn", [P, QT, D]), sb("xT", [P, DC, S])
        stats, mean_var, rstd = sb("stats", [P, QT, 6]), sb("mean_var", [P, QT, 2]), sb("rstd", [P, QT, 2])
        c_s, cT = sb("c_s", [P, KT, D]), sb("cT", [P, DC, SK])
        kp, krest = sb("kp", [P, PARTS, DC, SK], BF16), sb("krest", [P, DC, SK])
        qp, qrest = sb("qp", [P, PARTS, DC, S], BF16), sb("qrest", [P, DC, S])
        vals = sb("vals", [P, KT, H, 2 * DH])
        m_s, bias, biasT = sb("m_s", [P, 2, SK], I32), sb("bias", [P, QT, SK], BF16), sb("biasT", [P, KT, S], BF16)
        w1_s = c_s[:, 0:FC, :]
        w2_s = m_s[:, :, 0:F].bitcast(F32)
        s1 = krest[:, 0, :].bitcast(BF16)[:, 0:FC * D].rearrange("p (c d) -> p c d", c=FC)
        s2 = krest[:, 1, :].bitcast(BF16)[:, 0:DC * F].rearrange("p (c d) -> p c d", c=DC)
        a1, a2 = w["a1"], sb("a2", [P, DC])
        ones16 = sb("ones16", [P, 2], BF16)
        masksum, maskodd, maskrow = sb("masksum", [1, SK]), sb("maskodd", [1, SK]), sb("maskrow", [1, SK], BF16)
        same = sb("same", [1, 2])
        fill = sb("fill", [DH, SK + S], BF16)
        ps = es.enter_context(nc.psum_tensor("ps1", [P, 8, 512], F32))
        psb = ps[:, :, :].bitcast(BF16)

        weights_in, ffn_in = sem("weights_in"), sem("ffn_in")
        ident_step, consts_ready = sem("ident_step"), sem("consts_ready")
        alpha_sum, alpha_ready, sign_ready = sem("alpha_sum"), sem("alpha_ready"), sem("sign_ready")
        ffn_tr, ffn_kept, alpha_out = sem("ffn_tr"), sem("ffn_kept"), sem("alpha_out")
        x_in, c_in, m_in = sem("x_in"), sem("c_in"), [sem("m_in0"), sem("m_in1")]
        ln_step, var_ready, std_ready, xn_ready = sem("ln_step"), sem("var_ready"), sem("std_ready"), sem("xn_ready")
        filled, act_freed, dve_freed = sem("filled"), sem("act_freed"), sem("dve_freed")
        hi_ready, rest_ready, mid_ready, lo_ready = sem("hi_ready"), sem("rest_ready"), sem("mid_ready"), sem("lo_ready")
        bias_ready, wait_carrier = sem("bias_ready"), sem("wait_carrier1")
        row_step, row_out, fill_out = sem("row_step"), sem("row_out"), sem("fill_out")
        k_out, q_out, v_out = sem("k_out"), sem("q_out"), sem("v_out")
        bias_out, biasT_out = sem("bias_out"), sem("biasT_out")

        jobs = [("cT", c, kb) for kb in range(len(KEY_BLOCKS)) for c in range(DC)]
        jobs += [("k", m, kb) for m in range(DC) for kb in range(len(KEY_BLOCKS))]
        pairs = list(range(0, KT, 2))
        for kt in pairs:
            jobs += [("v", kt, 0), ("m", kt, 0)]
            if kt // 2 >= 1 and kt // 2 <= len(KEY_BLOCKS):
                jobs += [("sum", 0, kt // 2 - 1)]
        jobs += [("xT", c, 0) for c in range(DC)]
        jobs += [("q", m, 0) for m in range(DC)]
        jobs_act = [j for j in jobs if j[0] in ("cT", "xT", "m", "sum")]
        jobs_dve = [j for j in jobs if j[0] in ("q", "k", "v")]
        splits = [j for j in jobs if j[0] in ("q", "k")]
        NJ, NA, NV, NS = len(jobs), len(jobs_act), len(jobs_dve), len(splits)
        NK = sum(j[0] == "k" for j in jobs)
        ROW_STEPS = 6

        def job_done(b, job):
            return b * NJ + jobs.index(job) + 1

        def bank_before(n):
            if n >= 8:
                return jobs[n - 8], False
            return [j for k, j in enumerate(jobs) if k % 8 == n][-1], True

        def first(b):
            return type(b) is int and b == 0

        def operand(kind, m, kb):
            if kind == "q":
                return qp, qrest, bq_s, m, 0, S
            return kp, krest, bk_s, m, KEY_BLOCKS[kb][0], KEY_BLOCKS[kb][1]

        with nc.Block() as block:
            @block.sync
            def _(sp):
                def load_rows(b):
                    if not first(b):
                        sp.wait_ge(filled, b * NJ - NJ + jobs.index(("cT", DC - 1, len(KEY_BLOCKS) - 1)) + 1)
                    sp.dma_start(c_s[:, 0:KT - 1, :], ctx_in[b, 0:(KT - 1) * P, :].rearrange("(t p) d -> p t d", p=P)).then_inc(c_in, 16)
                    sp.dma_start(c_s[0:KLAST, KT - 1, :], ctx_in[b, (KT - 1) * P:SK, :]).then_inc(c_in, 16)
                    if not first(b):
                        sp.wait_ge(xn_ready, b * QT)
                    sp.dma_start(x_s[:, :, :], x[b, :, :].rearrange("(t p) d -> p t d", p=P)).then_inc(x_in, 16)

                def store(b):
                    sp.wait_ge(bias_ready, b * QT + QT)
                    sp.dma_start(bias_d[b, :, :, :], bias[:, :, :]).then_inc(bias_out, 16)
                    for kind, parts, dram, out in (("k", kp, kparts_d, k_out), ("q", qp, qparts_d, q_out)):
                        if kind == "q":
                            store_values(b)
                        for m in range(DC):
                            sp.wait_ge(lo_ready, b * NS + splits.index((kind, m, len(KEY_BLOCKS) - 1 if kind == "k" else 0)) + 1)
                            for g in (2 * m, 2 * m + 1):
                                rows = slice(GR * (g % 2), GR * (g % 2) + GR)
                                for part in range(PARTS):
                                    sp.dma_start(dram[b * NG + g, part, :, :, :].rearrange("d h c -> h d c"),
                                                 parts[rows, part, m, :]).then_inc(out, 16)

                def store_values(b):
                    sp.wait_ge(dve_freed, b * NV + jobs_dve.index(("v", pairs[-1], 0)) + 1)
                    for g in range(NG):
                        sp.dma_start(values_d[b * NG + g, :, :, :],
                                     vals[:, :, HG * g:HG * (g + 1), :].rearrange("p t h c -> p t (h c)")).then_inc(v_out, 16)
                    sp.wait_ge(act_freed, b * NA + jobs_act.index(("m", pairs[-1], 0)) + 1)
                    sp.dma_start(biasT_d[b, :, :, :], biasT[:, :, :]).then_inc(biasT_out, 16)
                    sp.wait_ge(row_step, b * ROW_STEPS + ROW_STEPS)
                    sp.dma_start(maskrow_d[bass.ds(b, 1), :], maskrow[:, :]).then_inc(row_out, 16)

                load_rows(0)
                for dst, src in ((wk_s, wk), (wv_s, wv), (wq_s, wq)):
                    sp.dma_start(dst[:, :, :], src.rearrange("(c p) d -> p c d", p=P)).then_inc(weights_in, 16)
                for dst, src in ((bk_s, bk), (bq_s, bq)):
                    sp.dma_start(dst[:, :], src.rearrange("(c p) -> p c", p=P), allow_slow_non_contiguous=True).then_inc(weights_in, 16)
                sp.dma_start(bv_s[:, :], bv.rearrange("(a d) -> a d", a=1).to_broadcast([P, D])).then_inc(weights_in, 16)
                sp.wait_ge(consts_ready, 6)
                for h in range(HG):
                    sp.dma_start(ones_d[:, h, :], fill[:, 0:SK]).then_inc(fill_out, 16)
                    sp.dma_start(zeros_d[:, h, :], fill[:, SK:SK + S]).then_inc(fill_out, 16)
                load_rows(1)
                store(0)
                with nc.sync.Fori(1, B - 1) as b:
                    load_rows(b + 1)
                    store(b)
                sp.wait_ge(filled, (B - 1) * NJ + jobs.index(("cT", DC - 1, len(KEY_BLOCKS) - 1)) + 1)
                sp.dma_start(w1_s, w1.rearrange("(c p) d -> p c d", p=P)).then_inc(ffn_in, 16)
                sp.wait_ge(bias_ready, B * QT)
                sp.dma_start(w2_s, w2.rearrange("(c p) d -> p c d", p=P)).then_inc(ffn_in, 16)
                store(B - 1)
                sp.wait_ge(alpha_ready, 2)
                sp.dma_start(alpha2_d.rearrange("(c p) -> p c", p=P), a2[:, :], allow_slow_non_contiguous=True).then_inc(alpha_out, 16)
                sp.wait_ge(alpha_out, 16)
                sp.wait_ge(fill_out, 2 * HG * 16)
                sp.wait_ge(row_out, B * 16)
                sp.wait_ge(k_out, B * NG * PARTS * 16)
                sp.wait_ge(q_out, B * NG * PARTS * 16)
                sp.wait_ge(v_out, B * NG * 16)
                sp.wait_ge(bias_out, B * 16)
                sp.wait_ge(biasT_out, B * 16)

            @block.gpsimd
            def _(pool):
                nc.gpsimd.memset(w["ident"][:, :], 0.0).then_inc(ident_step, 1)
                nc.gpsimd.memset(w["ident16"][:, :], 0.0).then_inc(ident_step, 1)
                pool.wait_ge(ident_step, 2)
                for m in (w["ident"], w["ident16"]):
                    nc.gpsimd.affine_select(out=m[:, :], in_=m[:, :], compare_op=ALU.not_equal, fill=1.0, base=0,
                                            pattern=[[-1, P]], channel_multiplier=1).then_inc(consts_ready, 1)
                for qt in (0, 1):
                    pool.dma_start(m_s[:, qt, :], mask[0, qt * P:(qt + 1) * P, :]).then_inc(m_in[qt], 16)
                nc.gpsimd.memset(vals[:, :, :, :], 1.0).then_inc(consts_ready, 1)
                nc.gpsimd.memset(biasT[:, KT - 1, :], 0.0).then_inc(consts_ready, 1)
                nc.gpsimd.memset(ones16[:, :], 1.0).then_inc(consts_ready, 1)
                nc.gpsimd.memset(fill[:, 0:SK], 1.0).then_inc(ident_step, 1)
                nc.gpsimd.memset(fill[:, SK:SK + S], 0.0).then_inc(ident_step, 1)
                pool.wait_ge(ident_step, 4)
                nc.gpsimd.memset(fill[0:1, SK:SK + S], 1.0).then_inc(consts_ready, 1)

                def load_mask(b, qt):
                    pool.wait_ge(bias_ready, b * QT + qt - 1)
                    pool.dma_start(m_s[:, qt % 2, :], mask[b, qt * P:(qt + 1) * P, :]).then_inc(m_in[qt % 2], 16)

                def batch(b, final):
                    for n, (kind, m, kb) in enumerate(splits):
                        parts, rest, _, m, c0, cn = operand(kind, m, kb)
                        pool.wait_ge(mid_ready, b * NS + n + 1)
                        nc.gpsimd.tensor_tensor(parts[:, 2, m, c0:c0 + cn], rest[:, m, c0:c0 + cn],
                                                parts[:, 1, m, c0:c0 + cn], ALU.subtract).then_inc(lo_ready, 1)
                        if n in (1, 3):
                            load_mask(b, 2 + n // 2)
                        if n == NK - 1 and not final:
                            load_mask(b + 1, 0)
                            load_mask(b + 1, 1)

                batch(0, False)
                with nc.gpsimd.Fori(1, B - 1) as b:
                    batch(b, False)
                batch(B - 1, True)

            @block.scalar
            def _(act):
                def batch(b, final):
                    n_split = 0

                    def round_mid(n):
                        kind, m, kb = splits[n]
                        parts, rest, _, m, c0, cn = operand(kind, m, kb)
                        act.wait_ge(rest_ready, b * NS + n + 1)
                        nc.scalar.activation(parts[:, 1, m, c0:c0 + cn], rest[:, m, c0:c0 + cn], ACT.Copy).then_inc(mid_ready, 1)

                    for n, (kind, i, kb) in enumerate(jobs):
                        bank = n % 8
                        if final and (kind, i) == ("m", pairs[-1]):
                            act.wait_ge(ffn_in, 32)
                            act.wait_ge(lo_ready, (B - 1) * NS + NK)
                            nc.scalar.activation(s1, w1_s, ACT.Sign).then_inc(sign_ready, 1)
                            nc.scalar.activation(s2, w2_s, ACT.Sign).then_inc(sign_ready, 1)
                        if (kind, i) == ("v", 0):
                            act.wait_ge(var_ready, b + 1)
                            nc.scalar.activation(rstd[:, :, 0], rstd[:, :, 0], ACT.Sqrt).then_inc(std_ready, 1)
                        if kind == "v":
                            continue
                        act.wait_ge(filled, b * NJ + n + 1)
                        if kind == "cT":
                            k0, kn = KEY_BLOCKS[kb]
                            nc.scalar.activation(cT[:, i, k0:k0 + kn], ps[:, bank, 0:kn], ACT.Copy).then_inc(act_freed, 1)
                        elif kind == "sum":
                            if kb == 0:
                                act.wait_ge(row_step, b * ROW_STEPS)
                            k0, kn = KEY_BLOCKS[kb]
                            nc.scalar.activation(masksum[:, k0:k0 + kn], ps[0:1, bank, 0:kn], ACT.Copy, scale=1.0 / MASKED).then_inc(act_freed, 1)
                        elif kind == "xT":
                            nc.scalar.activation(xT[:, i, :], ps[:, bank, :], ACT.Copy).then_inc(act_freed, 1)
                        elif kind == "m":
                            act.wait_ge(biasT_out, b * 16)
                            if i == 0:
                                act.wait_ge(consts_ready, 6)
                            if i == KT - 1:
                                nc.scalar.activation(biasT[0:KLAST, i, :], psb[0:KLAST, bank, 0:S], ACT.Copy).then_inc(act_freed, 1)
                            else:
                                nc.scalar.activation(biasT[:, i:i + 2, :], psb[:, bank, :].rearrange("p (a s) -> p a s", a=2),
                                                     ACT.Copy).then_inc(act_freed, 1)
                        else:
                            parts, rest, bias_s, m, c0, cn = operand(kind, i, kb)
                            if (i, kb) == (0, 0):
                                act.wait_ge(k_out if kind == "k" else q_out, b * NG * PARTS * 16)
                                act.wait_ge(weights_in, 6 * 16)
                            nc.scalar.activation(parts[:, 0, m, c0:c0 + cn], ps[:, bank, 0:cn], ACT.Identity,
                                                 bias=bias_s[:, m:m + 1]).then_inc(hi_ready, 1)
                            if n_split not in (0, NK):
                                round_mid(n_split - 1)
                            n_split += 1
                            if n_split in (NK, NS):
                                round_mid(n_split - 1)

                batch(0, False)
                with nc.scalar.Fori(1, B - 1) as b:
                    batch(b, False)
                batch(B - 1, True)
                for n in range(2 * DC):
                    act.wait_ge(ffn_tr, n + 1)
                    dst = w["w1T"][:, n, :] if n < DC else w["w2T"][:, 4 * (n - DC):4 * (n - DC) + 4, :].rearrange("p a d -> p (a d)")
                    nc.scalar.activation(dst, psb[:, n, :], ACT.Copy).then_inc(ffn_kept, 1)

            @block.vector
            def _(v):
                v.wait_ge(weights_in, 6 * 16)
                v.wait_ge(consts_ready, 6)
                def batch(b):
                    v.wait_ge(bias_out, 16 * b)
                    converted = 0
                    n_split = 0
                    for n, (kind, i, kb) in enumerate(jobs):
                        bank = n % 8
                        if (kind, i) == ("v", 0):
                            layernorm(b)
                        if (kind, i) == ("xT", 0):
                            mask_row(b)
                        if kind in ("q", "k"):
                            parts, rest, bias_s, m, c0, cn = operand(kind, i, kb)
                            v.wait_ge(hi_ready, b * NS + n_split + 1)
                            nc.vector.scalar_tensor_tensor(rest[:, m, c0:c0 + cn], ps[:, bank, 0:cn], bias_s[:, m:m + 1],
                                                           parts[:, 0, m, c0:c0 + cn], ALU.add, ALU.subtract).then_inc(rest_ready, 1)
                            v.wait_ge(rest_ready, b * NS + n_split + 1)
                            v.sem_inc(dve_freed, 1)
                            n_split += 1
                            if n_split % 2 == 0 and converted < QT:
                                v.wait_ge(m_in[converted % 2], (b * (QT // 2) + converted // 2 + 1) * 16)
                                nc.vector.tensor_scalar(bias[:, converted, :], m_s[:, converted % 2, :], 0, MASKED,
                                                        ALU.is_equal, ALU.mult).then_inc(bias_ready, 1)
                                converted += 1
                        elif kind == "v":
                            v.wait_ge(filled, b * NJ + n + 1)
                            v.wait_ge(v_out, b * NG * 16)
                            tiles = 2 if i < KT - 1 else 1
                            r = P if i < KT - 1 else KLAST
                            for t in range(tiles):
                                last = nc.vector.tensor_tensor(
                                    vals[0:r, i + t, :, 0:DH],
                                    ps[0:r, bank, t * D:(t + 1) * D].rearrange("p (h c) -> p h c", h=H),
                                    bv_s[0:r, :].rearrange("p (h c) -> p h c", h=H), ALU.add)
                                if t == tiles - 1:
                                    last.then_inc(dve_freed, 1)

                def layernorm(b):
                    v.wait_ge(x_in, 16 * b + 16)
                    for t in range(QT):
                        nc.vector.bn_stats(stats[:, t, :], x_s[:, t, :]).then_inc(ln_step, 1)
                    v.wait_ge(ln_step, b * (2 * QT + 1) + QT)
                    v.sem_inc(wait_carrier, 1)
                    for t in range(QT):
                        nc.vector.bn_aggr(mean_var[:, t, :], stats[:, t, :]).then_inc(ln_step, 1)
                    v.wait_ge(ln_step, b * (2 * QT + 1) + 2 * QT)
                    layernorm_scales(nc, v, mean_var, rstd, var_ready, std_ready, ln_step, b * (2 * QT + 1) + 2 * QT + 1, b)
                    if not first(b):
                        v.wait_ge(filled, b * NJ - NJ + jobs.index(("xT", DC - 1, 0)) + 1)
                    for t in range(QT):
                        nc.vector.tensor_scalar(xn[:, t, :], x_s[:, t, :], mean_var[:, t, 0:1], rstd[:, t, 1:2],
                                                ALU.subtract, ALU.mult).then_inc(xn_ready, 1)

                def mask_row(b):
                    step = b * ROW_STEPS
                    v.wait_ge(act_freed, b * NA + jobs_act.index(("sum", 0, len(KEY_BLOCKS) - 1)) + 1)
                    v.wait_ge(row_out, b * 16)
                    nc.vector.scalar_tensor_tensor(maskodd[:, :], masksum[:, :], -float(S), masksum[:, :],
                                                   ALU.add, ALU.mult).then_inc(row_step, 1)
                    v.wait_ge(row_step, step + 1)
                    nc.vector.tensor_reduce(same[:, 0:1], maskodd[:, :], AX_X, ALU.min).then_inc(row_step, 1)
                    v.wait_ge(row_step, step + 2)
                    nc.vector.tensor_scalar(w["mixed"][:, bass.ds(b, 1)], same[:, 0:1], 0.0, None, ALU.is_lt).then_inc(row_step, 1)
                    nc.vector.tensor_scalar(same[:, 1:2], same[:, 0:1], 0.0, MASKED, ALU.is_ge, ALU.mult).then_inc(row_step, 1)
                    v.wait_ge(row_step, step + 4)
                    nc.vector.tensor_scalar(maskrow[:, :], masksum[:, :], float(S), None, ALU.is_equal).then_inc(row_step, 1)
                    v.wait_ge(row_step, step + 5)
                    nc.vector.tensor_scalar(maskrow[:, :], maskrow[:, :], same[:, 1:2], None, ALU.mult).then_inc(row_step, 1)

                batch(0)
                with nc.vector.Fori(1, B) as b:
                    batch(b)
                v.wait_ge(ffn_in, 32)
                nc.vector.tensor_reduce(a1[:, :], w1_s, AX_X, ALU.add, apply_absolute_value=True).then_inc(alpha_sum, 1)
                nc.vector.tensor_reduce(a2[:, :], w2_s, AX_X, ALU.add, apply_absolute_value=True).then_inc(alpha_sum, 1)
                v.wait_ge(alpha_sum, 2)
                nc.vector.tensor_scalar(a1[:, :], a1[:, :], 1.0 / D, None, ALU.mult).then_inc(alpha_ready, 1)
                nc.vector.tensor_scalar(a2[:, :], a2[:, :], 1.0 / F, None, ALU.mult).then_inc(alpha_ready, 1)

            @block.tensor
            def _(pe):
                pe.wait_ge(consts_ready, 2)

                def batch(b):
                    for n, (kind, i, kb) in enumerate(jobs):
                        bank = n % 8
                        before, earlier = bank_before(n)
                        if not (earlier and first(b)):
                            if before in jobs_act:
                                pe.wait_ge(act_freed, b * NA + (jobs_act.index(before) + 1 - NA * earlier))
                            else:
                                pe.wait_ge(dve_freed, b * NV + (jobs_dve.index(before) + 1 - NV * earlier))
                        if kind == "cT":
                            if n == 0:
                                pe.wait_ge(c_in, 32 * b + 32)
                            if n == 0 and not first(b):
                                pe.wait_ge(dve_freed, b * NV - NV + jobs_dve.index(("v", pairs[-1], 0)) + 1)
                            k0, kn = KEY_BLOCKS[kb]
                            for q in range(0, kn, P):
                                r = min(P, kn - q)
                                last = nc.tensor.transpose(ps[:, bank, q:q + r], c_s[0:r, (k0 + q) // P, i * P:(i + 1) * P],
                                                           w["ident"][0:r, 0:r])
                        elif kind == "xT":
                            pe.wait_ge(xn_ready, b * QT + QT)
                            for q in range(QT):
                                last = nc.tensor.transpose(ps[:, bank, q * P:(q + 1) * P], xn[:, q, i * P:(i + 1) * P], w["ident"][:, :])
                        elif kind == "q":
                            pe.wait_ge(act_freed, b * NA + jobs_act.index(("xT", DC - 1, 0)) + 1)
                            for c in range(DC):
                                last = nc.tensor.matmul(ps[:, bank, :], wq_s[:, c, i * P:(i + 1) * P], xT[:, c, :],
                                                        start=c == 0, stop=c == DC - 1)
                        elif kind == "k":
                            if first(b) and (i, kb) == (0, 0):
                                pe.wait_ge(weights_in, 6 * 16)
                            pe.wait_ge(act_freed, b * NA + jobs_act.index(("cT", DC - 1, kb)) + 1)
                            k0, kn = KEY_BLOCKS[kb]
                            for c in range(DC):
                                last = nc.tensor.matmul(ps[:, bank, 0:kn], wk_s[:, c, i * P:(i + 1) * P], cT[:, c, k0:k0 + kn],
                                                        start=c == 0, stop=c == DC - 1)
                        elif kind == "v":
                            for t in range(2 if i < KT - 1 else 1):
                                r = keys_in(i + t)
                                for c in range(DC):
                                    last = nc.tensor.matmul(ps[0:r, bank, t * D:(t + 1) * D], cT[:, c, (i + t) * P:(i + t) * P + r],
                                                            wv_s[:, c, :], start=c == 0, stop=c == DC - 1)
                        elif kind == "sum":
                            if first(b) and kb == 0:
                                pe.wait_ge(consts_ready, 6)
                            k0, kn = KEY_BLOCKS[kb]
                            for q in range(QT):
                                last = nc.tensor.matmul(ps[0:1, bank, 0:kn], ones16[:, 0:1], bias[:, q, k0:k0 + kn],
                                                        start=q == 0, stop=q == QT - 1)
                        else:
                            pe.wait_ge(bias_ready, b * QT + QT)
                            for t in range(2 if i < KT - 1 else 1):
                                r = keys_in(i + t)
                                for q in range(QT):
                                    last = nc.tensor.transpose(psb[0:r, bank, t * S + q * P:t * S + (q + 1) * P],
                                                               bias[:, q, (i + t) * P:(i + t) * P + r], w["ident16"][:, :])
                        last.then_inc(filled, 1)

                batch(0)
                with nc.tensor.Fori(1, B) as b:
                    batch(b)
                pe.wait_ge(sign_ready, 2)
                pe.wait_ge(act_freed, B * NA)
                pe.wait_ge(dve_freed, B * NV)
                for n in range(DC):
                    for c in range(FC):
                        last = nc.tensor.transpose(psb[:, n, c * P:(c + 1) * P], s1[:, c, n * P:(n + 1) * P], w["ident16"][:, :])
                    last.then_inc(ffn_tr, 1)
                for n in range(DC):
                    for q in range(8):
                        f, c = 4 * n + q // 2, q % 2
                        last = nc.tensor.transpose(psb[:, DC + n, q * P:(q + 1) * P], s2[:, c, f * P:(f + 1) * P], w["ident16"][:, :])
                    last.then_inc(ffn_tr, 1)


MC = QT * HG * NCH
EARLY = 10
LATE = 4


def order(next1, next2):
    chunks = [("C1", m) for m in range(EARLY, MC)] * next1 + [("C2", m) for m in range(EARLY)] * next2
    slots = 3 * KT
    due = {}
    for k, c in enumerate(chunks):
        due.setdefault(k * slots // MC, []).append(c)
    t_slot = (MC - EARLY - 1) * slots // MC + LATE
    steps, slot = [], 0

    def fill():
        nonlocal slot
        steps.extend(due.get(slot, []))
        if next1 and slot == t_slot:
            steps.append(("T", 0))
        slot += 1

    for kt in range(KT):
        steps.extend([("S", kt, 0), ("S", kt, 1)])
        fill()
        steps.extend([("S", kt, 2), ("S", kt, 3)])
        fill()
        steps.append(("V", kt - 1))
        fill()
    return steps


def units(steps):
    return [x for x in steps if x[0] in "ST"]


RING = 3
UNITS = KT * HG + 1
BATCH_UNITS = NG * UNITS


def attend(nc, w, g_attn, g_ffn, wo, bo, b1, b2, alpha2_d, kparts_d, qparts_d, values_d, bias_d, biasT_d, maskrow_d, ones_d, zeros_d,
           heads_d, sums_d, recips_d):
    with ExitStack() as es:
        def sb(name, shape, dt=F32):
            return es.enter_context(nc.sbuf_tensor(name, shape, dt))

        def sem(name):
            return es.enter_context(nc.semaphore(name))

        kst = [sb(f"kst{g}", [P, HG, SK], BF16) for g in range(NG)]
        qst = [sb(f"qst{g}", [P, HG, S], BF16) for g in range(NG)]
        vst = [sb(f"vst{g}", [P, KT, HG * 2 * DH]) for g in range(NG)]
        bias, biasT = sb("bias2", [P, QT, SK], BF16), sb("biasT2", [P, KT, S], BF16)
        PR = 3
        probs = sb("probs", [P, PR, HG, S])
        outs = sb("outs", [P, 2, S])
        junk = sb("junk", [P, 2, CW], BF16)
        cmax = sb("cmax", [P, 2, QT * HG, NCH])
        negmax, rest = sb("negmax", [P, 2, QT * HG]), sb("rest", [P, 2, QT * HG])
        mparts, mrows = sb("mparts", [P, P // (QT * HG), QT * HG], BF16), sb("mrows", [PARTS * QT * HG, P], BF16)
        wo_s, bo_s, gate, b1_s, b2_s = w["wo"], w["bo"], w["gate"], w["b1"], w["b2"]
        sums, recips = sb("sums2", [P, (B - 1) * H * S // P]), sb("recips2", [P, (B - 1) * H * S // P])
        ps_s = es.enter_context(nc.psum_tensor("ps_s", [P, RING, S], F32))
        ps_m = es.enter_context(nc.psum_tensor("ps_m", [P, 2, 2 * 512], F32))
        ps_o = es.enter_context(nc.psum_tensor("ps_o", [P, S], F32))
        ps_tr = ps_s[:, :, :].bitcast(BF16)

        mparts_init, wait_carrier = sem("mparts_init"), sem("wait_carrier")
        rows_in, mask_rows_in = sem("rows_in"), [sem(f"mask_rows_in{g}") for g in range(NG)]
        wo_zeroed, consts_in, gates_ready, biases_gated = sem("wo_zeroed"), sem("consts_in"), sem("gates_ready"), sem("biases_gated")
        stack_in = [sem(f"stack_in{g}") for g in range(NG)]
        values_in = [sem(f"values_in{g}") for g in range(NG)]
        bias_in = [sem(f"bias_in{t}") for t in range(QT)]
        biasT_in = sem("biasT_in")
        scored, freed, summed, out_kept = sem("scored"), sem("freed"), sem("summed"), sem("out_kept")
        out_stored = [sem("out_stored0"), sem("out_stored1")]
        max_scored, max_taken = sem("max_scored"), sem("max_taken")
        max_step, max_parts, max_in = sem("max_step"), sem("max_parts"), sem("max_in")
        sums_in, recips_step, recips_out = sem("sums_in"), sem("recips_step"), sem("recips_out")
        NDMA = 2 * len(STACK) - 2 + 1
        STEPS = 6

        def group_steps(last, g):
            return order(not (last and g == NG - 1), not (last and g >= NG - 2))

        def unit_base(b):
            return b * BATCH_UNITS + 1

        def transposed_unit(b, g, last):
            return unit_base(b) + g * UNITS + units(group_steps(last, g)).index(("T", 0)) + 1

        def batch_of(b, g):
            return b if g < NG else b + 1

        def load_parts(sp, g, gi):
            def rows(t, r0, r1):
                return t[r0:r1, :, :].rearrange("p h c -> p (h c)")

            kd, qd = kparts_d[gi, :, :, :, :].rearrange("a d h c -> (a d) (h c)"), qparts_d[gi, :, :, :, :].rearrange("a d h c -> (a d) (h c)")
            for dst, r0, r1, src, s0 in ((kst[g], 0, 16, kd, 0), (kst[g], 32, 64, kd, DH), (kst[g], 64, 96, kd, 0), (kst[g], 96, 112, kd, 0),
                                         (qst[g], 0, 16, qd, 0), (qst[g], 32, 48, qd, 0), (qst[g], 48, 64, qd, 0),
                                         (qst[g], 64, 80, qd, DH), (qst[g], 80, 96, qd, DH), (qst[g], 96, 112, qd, 2 * DH)):
                sp.dma_start(rows(dst, r0, r1), src[s0:s0 + r1 - r0, :]).then_inc(stack_in[g], 16)

        def load_mask_row(sp, g, b):
            mrow = maskrow_d[bass.ds(b, 1), :].rearrange("a (h c) -> a h c", h=1).to_broadcast([1, HG, SK])
            sp.dma_start(kst[g][MASK_ROW:MASK_ROW + 1, :, :], mrow).then_inc(stack_in[g], 16)

        def load_values(sp, g, gi):
            sp.dma_start(vst[g][:, :, :], values_d[gi, :, :, :]).then_inc(values_in[g], 16)

        def max_rows_in(sp, g, copied):
            sp.wait_ge(freed, copied)
            for p in range(PARTS):
                sp.dma_start(qst[g][MAX_ROW + p:MAX_ROW + p + 1, :, :].rearrange("p h c -> p (h c)"),
                             mrows[p * QT * HG:(p + 1) * QT * HG, :]).then_inc(max_in, 16)

        with nc.Block() as block:
            @block.sync
            def _(sp):
                for g in range(NG):
                    load_parts(sp, g, g)
                    sp.wait_ge(mask_rows_in[g], 32)
                    load_mask_row(sp, g, 0)
                    load_values(sp, g, g)
                sp.wait_ge(wo_zeroed, 1)
                for g in range(NG):
                    for h in range(HG):
                        r0 = (g * HG + h) * DH
                        sp.dma_start(wo_s[2 * DH * h:2 * DH * h + DH, g, :], wo[r0:r0 + DH, :]).then_inc(consts_in, 16)
                for dst, src in ((bo_s, bo), (b2_s, b2), (w["a2"], alpha2_d)):
                    sp.dma_start(dst[:, :], src.rearrange("(a d) -> a d", a=1).to_broadcast([P, D])).then_inc(consts_in, 16)
                sp.dma_start(b1_s[:, :], b1.rearrange("(c p) -> p c", p=P), allow_slow_non_contiguous=True).then_inc(consts_in, 16)
                for k, src in enumerate((g_attn, g_ffn)):
                    sp.dma_start(gate[:, k:k + 1], src.rearrange("(a d) -> a d", a=1).to_broadcast([P, 1])).then_inc(consts_in, 16)
                max_rows_in(sp, 0, 1)

                def batch(b, last):
                    for g in range(NG):
                        if not (last and g == NG - 1):
                            max_rows_in(sp, (g + 1) % NG, transposed_unit(b, g, last))
                        if not last:
                            sp.wait_ge(summed, (b * NG + g + 1) * KT)
                            load_parts(sp, g, b * NG + g + NG)
                            load_mask_row(sp, g, b + 1)
                            load_values(sp, g, b * NG + g + NG)
                        if last and g == 1:
                            for stored in out_stored:
                                sp.wait_ge(stored, (B - 1) * NG // 2 * 32)
                            sp.dma_start(sums[:, :], sums_d[0:B - 1, :, :].rearrange("b h s -> (b h s)").rearrange("(p c) -> p c", p=P)).then_inc(sums_in, 16)
                            sp.wait_ge(recips_step, 1)
                            sp.dma_start(recips_d[0:B - 1, :, :].rearrange("b h s -> (b h s)").rearrange("(p c) -> p c", p=P), recips[:, :]).then_inc(recips_out, 16)

                batch(0, False)
                with nc.sync.Fori(1, B - 1) as b:
                    batch(b, False)
                batch(B - 1, True)
                sp.wait_ge(recips_out, 16)

            @block.gpsimd
            def _(pool):
                for qt in range(QT):
                    pool.dma_start(bias[:, qt, :], bias_d[0, :, qt, :]).then_inc(bias_in[qt], 16)
                pool.dma_start(biasT[:, :, :], biasT_d[0, :, :, :]).then_inc(biasT_in, 16)
                nc.gpsimd.memset(wo_s[:, :, :], 0.0).then_inc(wo_zeroed, 1)
                pool.wait_ge(gates_ready, 1)
                nc.gpsimd.tensor_scalar(bo_s[:, :], bo_s[:, :], gate[:, 0:1], None, ALU.mult).then_inc(biases_gated, 1)
                nc.gpsimd.tensor_scalar(b2_s[:, :], b2_s[:, :], gate[:, 1:2], None, ALU.mult).then_inc(biases_gated, 1)
                nc.gpsimd.tensor_scalar(w["a2"][:, :], w["a2"][:, :], gate[:, 1:2], None, ALU.mult).then_inc(biases_gated, 1)

                def store(b, g):
                    pool.wait_ge(out_kept, b * NG + g + 1)
                    pool.dma_start(heads_d[b * NG + g, :, :], outs[:, g % 2, :]).then_inc(out_stored[g % 2], 16)
                    pool.dma_start(sums_d[b, g * HG:(g + 1) * HG, :], outs[DH::2 * DH, g % 2, :]).then_inc(out_stored[g % 2], 16)

                def next_bias(b, qt):
                    pool.wait_ge(max_taken, (b * NG + NG - 1) * MC + (qt + 1) * HG * NCH)
                    pool.dma_start(bias[:, qt, :], bias_d[b + 1, :, qt, :]).then_inc(bias_in[qt], 16)

                def batch(b, last):
                    store(b, 0)
                    if not last:
                        next_bias(b, 0)
                    store(b, 1)
                    if not last:
                        for qt in range(1, QT):
                            next_bias(b, qt)
                    store(b, 2)
                    store(b, 3)
                    if not last:
                        pool.wait_ge(scored, unit_base(b + 1))
                        pool.dma_start(biasT[:, :, :], biasT_d[b + 1, :, :, :]).then_inc(biasT_in, 16)

                batch(0, False)
                with nc.gpsimd.Fori(1, B - 1) as b:
                    batch(b, False)
                batch(B - 1, True)
                for stored in out_stored:
                    pool.wait_ge(stored, B * NG // 2 * 32)

            @block.scalar
            def _(act):
                for g in range(NG):
                    if g == 1:
                        act.wait_ge(stack_in[0], NDMA * 16)
                    act.dma_start(kst[g][MASK_ROW:MASK_ROW + DH, :, :], ones_d[:, :, :]).then_inc(mask_rows_in[g], 16)
                    act.dma_start(qst[g][MASK_ROW:MASK_ROW + DH, :, :], zeros_d[:, :, :]).then_inc(mask_rows_in[g], 16)
                for g in range(NG):
                    act.dma_start(kst[g][MAX_ROW:MAX_ROW + DH, :, :], ones_d[:, :, :]).then_inc(rows_in, 16)
                    act.dma_start(qst[g][MAX_ROW + PARTS:P, :, :], zeros_d[1:1 + P - MAX_ROW - PARTS, :, :]).then_inc(rows_in, 16)

                def copy_maxima(b_unit, n):
                    act.wait_ge(scored, b_unit + n + 1)
                    nc.scalar.activation(mrows[:, :], ps_tr[0:PARTS * QT * HG, n % RING, 0:P], ACT.Copy).then_inc(freed, 1)

                copy_maxima(0, 0)
                act.wait_ge(consts_in, (NG * HG + 6) * 16)
                nc.scalar.activation(gate[:, :], gate[:, :], ACT.Tanh).then_inc(gates_ready, 1)

                def batch(b, last):
                    n = 0
                    for g in range(NG):
                        for step in units(group_steps(last, g)):
                            if step[0] == "T":
                                act.wait_ge(max_in, (b * NG + g + 1) * PARTS * 16)
                                copy_maxima(unit_base(b), n)
                            else:
                                kt, h = step[1:]
                                tile, r = g * KT + kt, keys_in(kt)
                                act.wait_ge(scored, unit_base(b) + n + 1)
                                if h == 0:
                                    act.wait_ge(summed, b * NG * KT + max(tile - PR + 1, 0))
                                nc.scalar.activation(probs[0:r, tile % PR, h, :], ps_s[0:r, n % RING, :],
                                                     ACT.Exp, scale=SCALE).then_inc(freed, 1)
                            n += 1

                batch(0, False)
                with nc.scalar.Fori(1, B - 1) as b:
                    batch(b, False)
                batch(B - 1, True)

            @block.vector
            def _(v):
                def take_max(g, gi, bi, m):
                    qt, h, c = m // (HG * NCH), (m // NCH) % HG, m % NCH
                    c0, cn = CHUNKS[c]
                    if m % (HG * NCH) == 0:
                        v.wait_ge(bias_in[qt], bi * 16 + 16)
                    v.wait_ge(max_scored, gi * MC + m + 1)
                    v.sem_inc(wait_carrier, 1)
                    nc.vector.tensor_tensor_reduce(junk[:, m % 2, 0:cn], ps_m[:, m % 2, 0:cn], bias[:, qt, c0:c0 + cn], 1.0, LOWEST,
                                                   ALU.add, ALU.max, cmax[:, g % 2, h * QT + qt, c:c + 1]).then_inc(max_taken, 1)

                def split_max(g, gi):
                    base = gi * STEPS
                    v.wait_ge(max_taken, (gi + 1) * MC)
                    nc.vector.tensor_reduce(negmax[:, 0, :], cmax[:, g % 2, :, :], AX_X, ALU.max).then_inc(max_step, 1)
                    v.wait_ge(max_step, base + 1)
                    nc.vector.tensor_scalar(negmax[:, 1, :], negmax[:, 0, :], MASKED, -1.0, ALU.max, ALU.mult).then_inc(max_step, 1)
                    v.wait_ge(max_in, gi * PARTS * 16)
                    v.wait_ge(max_step, base + 2)
                    nc.vector.tensor_copy(mparts[:, 0, :], negmax[:, 1, :]).then_inc(max_step, 1)
                    v.wait_ge(max_step, base + 3)
                    nc.vector.tensor_tensor(rest[:, 0, :], negmax[:, 1, :], mparts[:, 0, :], ALU.subtract).then_inc(max_step, 1)
                    v.wait_ge(max_step, base + 4)
                    nc.vector.tensor_copy(mparts[:, 1, :], rest[:, 0, :]).then_inc(max_step, 1)
                    v.wait_ge(max_step, base + 5)
                    nc.vector.tensor_tensor(rest[:, 1, :], rest[:, 0, :], mparts[:, 1, :], ALU.subtract).then_inc(max_step, 1)
                    v.wait_ge(max_step, base + 6)
                    nc.vector.tensor_copy(mparts[:, 2, :], rest[:, 1, :]).then_inc(max_parts, 1)

                def keep_output(b, g):
                    v.wait_ge(summed, (b * NG + g + 1) * KT)
                    v.wait_ge(out_stored[g % 2], (b * (NG // 2) + g // 2) * 32)
                    nc.vector.tensor_copy(outs[:, g % 2, :], ps_o[:, :]).then_inc(out_kept, 1)

                nc.vector.memset(mparts[:, :, :], 0.0).then_inc(mparts_init, 1)
                v.wait_ge(mparts_init, 1)
                for m in range(MC):
                    take_max(0, 0, 0, m)
                split_max(0, 0)
                for m in range(EARLY):
                    take_max(1, 1, 0, m)

                def batch(b, last):
                    for g in range(NG):
                        gi = b * NG + g
                        next1, next2 = not (last and g == NG - 1), not (last and g >= NG - 2)
                        for m in range(EARLY, MC) if next1 else ():
                            take_max((g + 1) % NG, gi + 1, batch_of(b, g + 1), m)
                            if g > 0 and m == EARLY + 2:
                                keep_output(b, g - 1)
                        if not next1:
                            keep_output(b, g - 1)
                        if next1:
                            split_max((g + 1) % NG, gi + 1)
                        for m in range(EARLY) if next2 else ():
                            take_max((g + 2) % NG, gi + 2, batch_of(b, g + 2), m)
                        if last and g == 1:
                            v.wait_ge(sums_in, 16)
                            nc.vector.reciprocal(recips[:, :], sums[:, :]).then_inc(recips_step, 1)
                    keep_output(b, NG - 1)

                batch(0, False)
                with nc.vector.Fori(1, B - 1) as b:
                    batch(b, False)
                batch(B - 1, True)

            @block.tensor
            def _(pe):
                def score_for_max(g, gi, bi, m):
                    if m == 0:
                        pe.wait_ge(stack_in[g], bi * NDMA * 16 + NDMA * 16)
                    if not (type(gi) is int and gi * MC + m < 2):
                        pe.wait_ge(max_taken, gi * MC + m - 1)
                    qt, h, c = m // (HG * NCH), (m // NCH) % HG, m % NCH
                    c0, cn = CHUNKS[c]
                    for a in range(0, cn, 512):
                        an = min(512, cn - a)
                        last = nc.tensor.matmul(ps_m[:, m % 2, a:a + an], qst[g][0:MAX_ROW, h, qt * P:(qt + 1) * P],
                                                kst[g][0:MAX_ROW, h, c0 + a:c0 + a + an], start=True, stop=True)
                    last.then_inc(max_scored, 1)

                def take_bank(b_unit, n):
                    pe.wait_ge(freed, b_unit + max(n - RING + 1, 0))

                def transpose_max(gi, n):
                    pe.wait_ge(max_parts, gi + 1)
                    nc.tensor.transpose(ps_tr[:, n % RING, 0:P], mparts[:, :, :].rearrange("p a n -> p (a n)"),
                                        w["ident16"][:, :]).then_inc(scored, 1)

                def score(g, kt, h, n, mixed):
                    r = keys_in(kt)
                    last = nc.tensor.matmul(ps_s[0:r, n % RING, :], kst[g][:, h, kt * P:kt * P + r], qst[g][:, h, :],
                                            start=True, stop=not mixed)
                    if mixed:
                        last = nc.tensor.matmul(ps_s[0:r, n % RING, :], w["ident16"][0:r, 0:r], biasT[0:r, kt, :],
                                                start=False, stop=True)
                    last.then_inc(scored, 1)

                def sum_tile(b, g, kt, tile, exps):
                    r = keys_in(kt)
                    pe.wait_ge(freed, exps)
                    if kt == 0:
                        pe.wait_ge(values_in[g], b * 16 + 16)
                        pe.wait_ge(out_kept, b * NG + g)
                    for h in range(HG):
                        strip = slice(2 * DH * h, 2 * DH * (h + 1))
                        last = nc.tensor.matmul(ps_o[strip, :], vst[g][0:r, kt, strip], probs[0:r, tile % PR, h, :],
                                                start=kt == 0, stop=kt == KT - 1)
                    last.then_inc(summed, 1)

                for m in range(MC):
                    score_for_max(0, 0, 0, m)
                transpose_max(0, 0)
                for m in range(EARLY):
                    score_for_max(1, 1, 0, m)

                def batch(b, last, mixed):
                    n, tail = 0, {}
                    if mixed:
                        pe.wait_ge(biasT_in, b * 16 + 16)
                    for g in range(NG):
                        gi = b * NG + g
                        pe.wait_ge(max_in, (gi + 1) * PARTS * 16)
                        for step in group_steps(last, g):
                            if step[0] == "S":
                                take_bank(unit_base(b), n)
                                score(g, step[1], step[2], n, mixed)
                                n += 1
                                tail[g * KT + step[1]] = unit_base(b) + n
                            elif step[0] == "T":
                                take_bank(unit_base(b), n)
                                transpose_max(gi + 1, n)
                                n += 1
                            elif step[0] == "V":
                                tile = g * KT + step[1]
                                if tile >= 0:
                                    sum_tile(b, tile // KT, tile % KT, tile, tail[tile])
                            else:
                                ahead = int(step[0][1])
                                score_for_max((g + ahead) % NG, gi + ahead, batch_of(b, g + ahead), step[1])
                    sum_tile(b, NG - 1, KT - 1, NG * KT - 1, tail[NG * KT - 1])

                pe.wait_ge(rows_in, NG * 32)

                def either(b, last):
                    mixed = nc.tensor.value_load(w["mixed"][0:1, bass.ds(b, 1)], min_val=0, max_val=1)
                    with nc.tensor.If(mixed != 0):
                        batch(b, last, True)
                    with nc.tensor.Else():
                        batch(b, last, False)

                either(0, False)
                with nc.tensor.Fori(1, B - 1) as b:
                    either(b, False)
                either(B - 1, True)


def finish(nc, w, x, heads_d, sums_d, recips_d, out):
    with ExitStack() as es:
        def sb(name, shape, dt=F32):
            return es.enter_context(nc.sbuf_tensor(name, shape, dt))

        def sem(name):
            return es.enter_context(nc.semaphore(name))

        wo_s, bo_s, gate, b1_s, b2_s = w["wo"], w["bo"], w["gate"], w["b1"], w["b2"]
        sums, recips = sb("sums3", [P, H * S // P]), sb("recips3", [P, H * S // P])
        heads, recip = sb("heads", [P, 2, NG, S]), sb("recip", [P, 2, NG, S])
        x_s, xb = sb("x3", [P, 2, QT, D]), sb("xb3", [P, B, QT, D])
        x1, xn = sb("x1", [P, B, QT, D]), sb("xn3", [P, B, QT, D])
        stats, mean_var, rstd = sb("stats3", [P, QT, 6]), sb("mean_var3", [P, QT, 2]), sb("rstd3", [P, QT, 2])
        xT, xrest = sb("xT3", [P, 2, PARTS, DC, S], BF16), sb("xrest3", [P, DC, S])
        hT, h, hrest = sb("hT3", [P, 2, PARTS, FC, S], BF16), sb("h3", [P, 4, S]), sb("hrest3", [P, 4, S])
        y = sb("y3", [P, 2, QT, D])
        ps_y = es.enter_context(nc.psum_tensor("ps_y", [P, 2, S], F32))
        ps_t = es.enter_context(nc.psum_tensor("ps_xt", [P, 2, S], F32))
        ps_h = es.enter_context(nc.psum_tensor("ps_h", [P, 4, S], F32))

        init = sem("init3")
        sums_in, recips_ready, recips_out = sem("sums_in3"), sem("recips_ready"), sem("recips_out3")
        heads_in, x_in = [sem("heads_in0"), sem("heads_in1")], [sem("x_in0"), sem("x_in1")]
        scaled, projected, xb_ready, x1_ready = sem("scaled"), sem("projected"), sem("xb_ready"), sem("x1_ready")
        ln_step, var_ready, std_ready, xn_ready = sem("ln_step3"), sem("var_ready3"), sem("std_ready3"), sem("xn_ready3")
        xb2_ready, transposed, xT_ready, hidden, gelu_ready, added, y_ready, x_step, y_step = (
            sem("xb2_ready"), sem("transposed"), sem("xT_ready"), sem("hidden"), sem("gelu_ready"), sem("added"), sem("y_ready"), sem("x_step"), sem("y_step"))
        h_hi, h_rest, h_mid, h_lo = sem("h_hi"), sem("h_rest"), sem("h_mid"), sem("h_lo")
        y_out = [sem("y_out0"), sem("y_out1")]

        with nc.Block() as block:
            @block.sync
            def _(sp):
                def load_batch(b):
                    if b >= 2:
                        sp.wait_ge(projected, (b - 1) * QT)
                        sp.wait_ge(xb_ready, b - 1)
                    sp.dma_start(heads[:, b % 2, :, :], heads_d[b * NG:(b + 1) * NG, :, :].rearrange("g p c -> p g c")).then_inc(heads_in[b % 2], 16)
                    for h in range(HG):
                        src = recips_d[b, :, :].rearrange("(a g h) s -> a h g s", a=1, h=HG)[:, h, :, :].to_broadcast([DH, NG, S])
                        sp.dma_start(recip[2 * DH * h:2 * DH * h + DH, b % 2, :, :], src).then_inc(heads_in[b % 2], 16)
                    sp.dma_start(x_s[:, b % 2, :, :], x[b, :, :].rearrange("(t p) d -> p t d", p=P)).then_inc(x_in[b % 2], 16)

                sp.dma_start(sums[:, :], sums_d[B - 1, :, :].rearrange("h s -> (h s)").rearrange("(p c) -> p c", p=P)).then_inc(sums_in, 16)
                sp.wait_ge(init, 2)
                load_batch(0)
                load_batch(1)
                sp.wait_ge(recips_ready, 1)
                sp.dma_start(recips_d[B - 1, :, :].rearrange("h s -> (h s)").rearrange("(p c) -> p c", p=P), recips[:, :]).then_inc(recips_out, 16)
                load_batch(2)
                sp.wait_ge(recips_out, 16)
                load_batch(3)

            @block.gpsimd
            def _(pool):
                nc.gpsimd.memset(recip[:, 0, :, :], 0.0).then_inc(init, 1)

                def store(b):
                    pool.wait_ge(y_ready, (b + 1) * QT)
                    pool.dma_start(out[b, :, :].rearrange("(t p) d -> p t d", p=P), y[:, b % 2, :, :]).then_inc(y_out[b % 2], 16)

                def scale_heads(b):
                    pool.wait_ge(heads_in[b % 2], (HG + 1) * 16 * (b // 2) + (HG + 1) * 16)
                    for g in range(NG):
                        nc.gpsimd.tensor_tensor(heads[:, b % 2, g, :], heads[:, b % 2, g, :], recip[:, b % 2, g, :], ALU.mult).then_inc(scaled, 1)

                def add_biases(b):
                    pool.wait_ge(x_in[b % 2], 16 * (b // 2) + 16)
                    for t in range(QT):
                        last = nc.gpsimd.tensor_tensor(xb[:, b, t, :], x_s[:, b % 2, t, :], bo_s[:, :], ALU.add)
                    last.then_inc(xb_ready, 1)

                scale_heads(0)
                add_biases(0)
                for b in range(1, B):
                    scale_heads(b)
                    add_biases(b)
                for b in range(B):
                    pool.wait_ge(x1_ready, (b + 1) * QT)
                    for t in range(QT):
                        last = nc.gpsimd.tensor_tensor(xb[:, b, t, :], x1[:, b, t, :], b2_s[:, :], ALU.add)
                    last.then_inc(xb2_ready, 1)
                for b in range(B):
                    for f in range(FC):
                        pool.wait_ge(h_mid, b * FC + f + 1)
                        nc.gpsimd.tensor_tensor(hT[:, b % 2, 2, f, :], hrest[:, f % 4, :], hT[:, b % 2, 1, f, :], ALU.subtract).then_inc(h_lo, 1)
                    if b:
                        store(b - 1)
                store(B - 1)
                for stored in y_out:
                    pool.wait_ge(stored, B // 2 * 16)

            @block.scalar
            def _(act):
                for b in range(B):
                    act.wait_ge(var_ready, b + 1)
                    nc.scalar.activation(rstd[:, :, 0], rstd[:, :, 0], ACT.Sqrt).then_inc(std_ready, 1)
                for b in range(B):
                    for f in range(FC):
                        act.wait_ge(hidden, b * FC + f + 1)
                        if b * FC + f >= 4:
                            act.wait_ge(h_rest, b * FC + f - 3)
                        nc.scalar.activation(h[:, f % 4, :], ps_h[:, f % 4, :], ACT.Gelu, bias=b1_s[:, f:f + 1], scale=w["a1"][:, f:f + 1]).then_inc(gelu_ready, 1)

            @block.vector
            def _(v):
                nc.vector.memset(recip[:, 1, :, :], 0.0).then_inc(init, 1)
                v.wait_ge(sums_in, 16)
                nc.vector.reciprocal(recips[:, :], sums[:, :]).then_inc(recips_ready, 1)

                def layernorm(b):
                    v.wait_ge(xb_ready, b + 1)
                    for t in range(QT):
                        v.wait_ge(projected, b * QT + t + 1)
                        nc.vector.scalar_tensor_tensor(x1[:, b, t, :], ps_h[:, t, 0:D], gate[:, 0:1], xb[:, b, t, :],
                                                       ALU.mult, ALU.add).then_inc(x1_ready, 1)
                    base = b * (2 * QT + 1)
                    for t in range(QT):
                        v.wait_ge(x1_ready, b * QT + t + 1)
                        nc.vector.bn_stats(stats[:, t, :], x1[:, b, t, :]).then_inc(ln_step, 1)
                    v.wait_ge(ln_step, base + QT)
                    for t in range(QT):
                        nc.vector.bn_aggr(mean_var[:, t, :], stats[:, t, :]).then_inc(ln_step, 1)
                    v.wait_ge(ln_step, base + 2 * QT)
                    layernorm_scales(nc, v, mean_var, rstd, var_ready, std_ready, ln_step, base + 2 * QT + 1, b)
                    for t in range(QT):
                        nc.vector.tensor_scalar(xn[:, b, t, :], x1[:, b, t, :], mean_var[:, t, 0:1], rstd[:, t, 1:2],
                                                ALU.subtract, ALU.mult).then_inc(xn_ready, 1)

                def split_xT(b):
                    if b >= 2:
                        v.wait_ge(hidden, (b - 1) * FC)
                    for c in range(DC):
                        base = (b * DC + c) * 3
                        v.wait_ge(transposed, b * DC + c + 1)
                        nc.vector.tensor_copy(xT[:, b % 2, 0, c, :], ps_t[:, c, :]).then_inc(x_step, 1)
                        v.wait_ge(x_step, base + 1)
                        nc.vector.tensor_tensor(xrest[:, c, :], ps_t[:, c, :], xT[:, b % 2, 0, c, :], ALU.subtract).then_inc(x_step, 1)
                        v.wait_ge(x_step, base + 2)
                        nc.vector.tensor_copy(xT[:, b % 2, 1, c, :], xrest[:, c, :]).then_inc(x_step, 1)
                        v.wait_ge(x_step, base + 3)
                        nc.vector.tensor_tensor(xT[:, b % 2, 2, c, :], xrest[:, c, :], xT[:, b % 2, 1, c, :], ALU.subtract).then_inc(xT_ready, 1)

                def split_h(b):
                    if b >= 2:
                        v.wait_ge(added, (b - 1) * QT)
                    for f in range(FC):
                        n = b * FC + f
                        v.wait_ge(gelu_ready, n + 1)
                        nc.vector.tensor_copy(hT[:, b % 2, 0, f, :], h[:, f % 4, :]).then_inc(h_hi, 1)
                        v.wait_ge(h_hi, n + 1)
                        if n >= 4:
                            v.wait_ge(h_lo, n - 3)
                        nc.vector.tensor_tensor(hrest[:, f % 4, :], h[:, f % 4, :], hT[:, b % 2, 0, f, :], ALU.subtract).then_inc(h_rest, 1)
                        v.wait_ge(h_rest, n + 1)
                        nc.vector.tensor_copy(hT[:, b % 2, 1, f, :], hrest[:, f % 4, :]).then_inc(h_mid, 1)

                def add_up(b):
                    v.wait_ge(xb2_ready, b + 1)
                    if b >= 2:
                        v.wait_ge(y_out[b % 2], b // 2 * 16)
                    for t in range(QT):
                        v.wait_ge(added, b * QT + t + 1)
                        nc.vector.tensor_tensor(y[:, b % 2, t, :], ps_y[:, t % 2, 0:D], w["a2"][:, :], ALU.mult).then_inc(y_step, 1)
                        v.wait_ge(y_step, b * QT + t + 1)
                        nc.vector.tensor_tensor(y[:, b % 2, t, :], y[:, b % 2, t, :], xb[:, b, t, :], ALU.add).then_inc(y_ready, 1)

                for b in range(B):
                    layernorm(b)
                    if b == 1:
                        split_xT(0)
                for b in range(B):
                    if b + 1 < B:
                        split_xT(b + 1)
                    split_h(b)
                    if b:
                        add_up(b - 1)
                add_up(B - 1)

            @block.tensor
            def _(pe):
                def project(b):
                    pe.wait_ge(scaled, (b + 1) * NG)
                    for t in range(QT):
                        if b:
                            pe.wait_ge(x1_ready, b * QT + t - 3)
                        for g in range(NG):
                            last = nc.tensor.matmul(ps_h[:, t, 0:D], heads[:, b % 2, g, t * P:(t + 1) * P], wo_s[:, g, :],
                                                    start=g == 0, stop=g == NG - 1)
                        last.then_inc(projected, 1)

                def transposes(b):
                    pe.wait_ge(xn_ready, (b + 1) * QT)
                    if b:
                        pe.wait_ge(xT_ready, b * DC)
                    for c in range(DC):
                        for t in range(QT):
                            last = nc.tensor.transpose(ps_t[:, c, t * P:(t + 1) * P], xn[:, b, t, c * P:(c + 1) * P], w["ident"][:, :])
                        last.then_inc(transposed, 1)

                def widen(b):
                    pe.wait_ge(xT_ready, (b + 1) * DC)
                    for f in range(FC):
                        if b * FC + f >= 4:
                            pe.wait_ge(gelu_ready, b * FC + f - 3)
                        elif f == 0:
                            pe.wait_ge(x1_ready, B * QT)
                        for c in range(DC):
                            for part in range(PARTS):
                                last = nc.tensor.matmul(ps_h[:, f % 4, :], w["w1T"][:, c, f * P:(f + 1) * P], xT[:, b % 2, part, c, :],
                                                        start=c == 0 and part == 0, stop=c == DC - 1 and part == PARTS - 1)
                        last.then_inc(hidden, 1)

                def narrow(b):
                    pe.wait_ge(h_lo, (b + 1) * FC)
                    for t in range(QT):
                        if b * QT + t >= 2:
                            pe.wait_ge(y_step, b * QT + t - 1)
                        for f in range(FC):
                            for part in range(PARTS):
                                last = nc.tensor.matmul(ps_y[:, t % 2, 0:D], hT[:, b % 2, part, f, t * P:(t + 1) * P], w["w2T"][:, f, :],
                                                        start=f == 0 and part == 0, stop=f == FC - 1 and part == PARTS - 1)
                        last.then_inc(added, 1)

                for b in range(B):
                    project(b)
                    if b == 1:
                        transposes(0)
                for b in range(B):
                    if b + 1 < B:
                        transposes(b + 1)
                    widen(b)
                    if b:
                        narrow(b - 1)
                narrow(B - 1)


def gated_cross_attention_block(nc, x, ctx_in, mask, g_attn, g_ffn, wq, bq, wk, bk, wv, bv, wo, bo, w1, b1, w2, b2, out):
    def dram(name, shape, dt=F32):
        return nc.dram_tensor(name, shape, dt, kind="Internal").ap()

    kparts_d = dram("kparts_d", (B * NG, PARTS, DH, HG, SK), BF16)
    qparts_d = dram("qparts_d", (B * NG, PARTS, DH, HG, S), BF16)
    values_d = dram("values_d", (B * NG, P, KT, HG * 2 * DH))
    bias_d = dram("bias_d", (B, P, QT, SK), BF16)
    biasT_d = dram("biasT_d", (B, P, KT, S), BF16)
    heads_d = dram("heads_d", (B * NG, P, S))
    alpha2_d = dram("alpha2_d", (D,))
    sums_d, recips_d = dram("sums_d", (B, H, S)), dram("recips_d", (B, H, S))
    ones_d, zeros_d = dram("ones_d", (DH, HG, SK), BF16), dram("zeros_d", (DH, HG, S), BF16)
    maskrow_d = dram("maskrow_d", (B, SK), BF16)
    with ExitStack() as es:
        w = {
            "ident": es.enter_context(nc.sbuf_tensor("ident", [P, P], F32)),
            "ident16": es.enter_context(nc.sbuf_tensor("ident16", [P, P], BF16)),
            "wo": es.enter_context(nc.sbuf_tensor("wo_s", [P, NG, D], F32)),
            "bo": es.enter_context(nc.sbuf_tensor("bo_s", [P, D], F32)),
            "gate": es.enter_context(nc.sbuf_tensor("gate", [P, 2], F32)),
            "b1": es.enter_context(nc.sbuf_tensor("b1_s", [P, FC], F32)),
            "b2": es.enter_context(nc.sbuf_tensor("b2_s", [P, D], F32)),
            "a1": es.enter_context(nc.sbuf_tensor("a1", [P, FC], F32)),
            "a2": es.enter_context(nc.sbuf_tensor("a2row", [P, D], F32)),
            "mixed": es.enter_context(nc.sbuf_tensor("mixed", [1, B], I32)),
            "w1T": es.enter_context(nc.sbuf_tensor("w1T", [P, DC, F], BF16)),
            "w2T": es.enter_context(nc.sbuf_tensor("w2T", [P, FC, D], BF16)),
        }
        prepare(nc, w, x, ctx_in, mask, wq, bq, wk, bk, wv, bv, w1, w2, alpha2_d, kparts_d, qparts_d, values_d, bias_d, biasT_d, maskrow_d,
                ones_d, zeros_d)
        attend(nc, w, g_attn, g_ffn, wo, bo, b1, b2, alpha2_d, kparts_d, qparts_d, values_d, bias_d, biasT_d, maskrow_d, ones_d, zeros_d,
               heads_d, sums_d, recips_d)
        finish(nc, w, x, heads_d, sums_d, recips_d, out)


_INS = ["x", "ctx_1024", "mask_BxSxS2_ik1", "g_xattn", "g_ffn", "L0_xattn_Wq", "L0_xattn_bq", "L0_xattn_Wk", "L0_xattn_bk",
        "L0_xattn_Wv", "L0_xattn_bv", "L0_xattn_Wo", "L0_xattn_bo", "L0_ffn_w1", "L0_ffn_b1", "L0_ffn_w2", "L0_ffn_b2"]


def kernel(**inputs):
    import numpy as _np
    import concourse.bacc as _bacc
    from concourse import mybir as _mybir
    from concourse.bass_utils import run_bass_kernel_spmd as _run

    nc = _bacc.Bacc("TRN2", target_bir_lowering=False, num_devices=1)
    arrays, args = {}, []
    for name in _INS:
        a = _np.ascontiguousarray(inputs[name])
        arrays[f"in_{name}_dram"] = a
        args.append(nc.dram_tensor(f"in_{name}_dram", a.shape, _mybir.dt.from_np(a.dtype), kind="ExternalInput").ap())
    args.append(nc.dram_tensor("out_0_dram", (B, S, D), F32, kind="ExternalOutput").ap())
    gated_cross_attention_block(nc, *args)
    r = _run(nc, [arrays], core_ids=[0])
    return r.results[0]["out_0_dram"]
```
